# Optimizing a Trainium2 kernel written in Bass

```python
import numpy as np
import jax
import jax.numpy as jnp

def _softmax(x, axis=-1):
    return jax.nn.softmax(x, axis=axis)

def _gelu(x):
    return jax.nn.gelu(x, approximate=True)

def _silu(x):
    return jax.nn.silu(x)

def _sigmoid(x):
    return jax.nn.sigmoid(x)

def _layernorm(x, axis=-1, eps=1e-05):
    m = jnp.mean(x, axis=axis, keepdims=True)
    v = jnp.var(x, axis=axis, keepdims=True)
    return (x - m) / jnp.sqrt(v + eps)

def _scatter_add(tgt, idx, src, axis=0):
    return tgt.at[idx].add(src)

def _segment_sum(src, seg, n):
    return jax.ops.segment_sum(src, seg, n)
kernel_name = 'mk_gnn_preln_d2_gnn_r32_5983df'

def setup_inputs(seed: int=0):
    np.random.seed(seed)
    _w = jnp.asarray

    def _rec_inputs():
        import jax
        import jax.numpy as jnp
        _gk = jax.random.key(seed)
        x = -0.0003713 + 1 * jax.random.normal(jax.random.fold_in(_gk, 1), (3125, 128), jnp.float32)
        src = jax.random.randint(jax.random.fold_in(_gk, 2), (50000,), 0, 3125, jnp.int32)
        dst = jax.random.randint(jax.random.fold_in(_gk, 3), (50000,), 0, 3125, jnp.int32)
        _o = jnp.argsort(dst, stable=True)
        src = src[_o]
        dst = dst[_o]
        edge_attr_4 = jax.random.uniform(jax.random.fold_in(_gk, 11), (50000, 4), jnp.float32, 0.0, 1)
        edge_weight = jax.random.uniform(jax.random.fold_in(_gk, 13), (50000,), jnp.float32, 0.0, 0.999998)
        return (x, src, dst, edge_attr_4, edge_weight)
    x, src, dst, edge_attr_4, edge_weight = _rec_inputs()

    def _L0_gnn_setup():
        import jax, jax.numpy as jnp
        import numpy as np
        N_NODES = 3125
        N_EDGES = 50000
        HIDDEN = 128
        N_ETYPES = 4
        N_STEPS = 4

        def _gru_cell(x, h, W_ih, W_hh, b_ih, b_hh):
            gi = x @ W_ih.T + b_ih
            gh = h @ W_hh.T + b_hh
            ir, iz, inn = jnp.split(gi, 3, axis=1)
            hr, hz, hn = jnp.split(gh, 3, axis=1)
            r = jax.nn.sigmoid(ir + hr)
            z = jax.nn.sigmoid(iz + hz)
            n = jnp.tanh(inn + r * hn)
            return (1.0 - z) * n + z * h
        key = jax.random.key(seed)
        ks = jax.random.split(key, 10)
        s = 1.0 / np.sqrt(HIDDEN)
        node_feat = jax.random.normal(ks[0], (N_NODES, HIDDEN), dtype=jnp.float32)
        edge_index = jax.random.randint(ks[1], (2, N_EDGES), 0, N_NODES)
        edge_feat = jax.random.uniform(ks[2], (N_EDGES, N_ETYPES), dtype=jnp.float32)
        W_edge = jax.random.uniform(ks[3], (N_ETYPES, HIDDEN, HIDDEN), minval=-s, maxval=s, dtype=jnp.float32)
        b_edge = jax.random.uniform(ks[4], (N_ETYPES, HIDDEN), minval=-s, maxval=s, dtype=jnp.float32)
        W_ih = jax.random.uniform(ks[5], (3 * HIDDEN, HIDDEN), minval=-s, maxval=s, dtype=jnp.float32)
        W_hh = jax.random.uniform(ks[6], (3 * HIDDEN, HIDDEN), minval=-s, maxval=s, dtype=jnp.float32)
        b_ih = jax.random.uniform(ks[7], (3 * HIDDEN,), minval=-s, maxval=s, dtype=jnp.float32)
        b_hh = jax.random.uniform(ks[8], (3 * HIDDEN,), minval=-s, maxval=s, dtype=jnp.float32)
        return {'node_feat': node_feat, 'edge_index': edge_index, 'edge_feat': edge_feat, 'W_edge': W_edge, 'b_edge': b_edge, 'W_ih': W_ih, 'W_hh': W_hh, 'b_ih': b_ih, 'b_hh': b_hh}
    _L0_gnn_all = _L0_gnn_setup()
    _L0_gnn_in = {k: v for k, v in _L0_gnn_all.items() if k in ('W_edge', 'b_edge', 'W_ih', 'W_hh', 'b_ih', 'b_hh')}
    del _L0_gnn_all

    def _L1_gnn_setup():
        import jax, jax.numpy as jnp
        import numpy as np
        N_NODES = 50000
        N_EDGES = 25000
        IN_F = 128
        OUT_F = 32
        HEADS = 4
        NEG_SLOPE = 0.2
        EPS = 1e-16
        key = jax.random.key(seed)
        k1, k2, k3, k4, k5 = jax.random.split(key, 5)
        x = jax.random.normal(k1, (N_NODES, IN_F), dtype=jnp.float32)
        edge_index = jax.random.randint(k2, (2, N_EDGES), 0, N_NODES, dtype=jnp.int64)
        edge_weights = jax.random.uniform(k3, (N_EDGES,), dtype=jnp.float32)
        lim_w = 1.0 / np.sqrt(IN_F)
        W = jax.random.uniform(k4, (HEADS, IN_F, OUT_F), dtype=jnp.float32, minval=-lim_w, maxval=lim_w)
        lim_a = np.sqrt(6.0 / (2 * OUT_F + 1))
        a = jax.random.uniform(k5, (HEADS, 2 * OUT_F), dtype=jnp.float32, minval=-lim_a, maxval=lim_a)
        return {'x': x, 'edge_index': edge_index, 'edge_weights': edge_weights, 'W': W, 'a': a}
    _L1_gnn_all = _L1_gnn_setup()
    _L1_gnn_in = {k: v for k, v in _L1_gnn_all.items() if k in ('W', 'a')}
    del _L1_gnn_all
    return {'x': x, 'src': src, 'dst': dst, 'edge_attr_4': edge_attr_4, 'edge_weight': edge_weight, 'L0_gnn_W_edge': _L0_gnn_in['W_edge'], 'L0_gnn_b_edge': _L0_gnn_in['b_edge'], 'L0_gnn_W_ih': _L0_gnn_in['W_ih'], 'L0_gnn_W_hh': _L0_gnn_in['W_hh'], 'L0_gnn_b_ih': _L0_gnn_in['b_ih'], 'L0_gnn_b_hh': _L0_gnn_in['b_hh'], 'L1_gnn_W': _L1_gnn_in['W'], 'L1_gnn_a': _L1_gnn_in['a']}

def reference(x, src, dst, edge_attr_4, edge_weight, L0_gnn_W_edge, L0_gnn_b_edge, L0_gnn_W_ih, L0_gnn_W_hh, L0_gnn_b_ih, L0_gnn_b_hh, L1_gnn_W, L1_gnn_a):
    import jax
    import jax.numpy as jnp

    def _L0_gnn_ref(node_feat, edge_index, edge_feat, W_edge, b_edge, W_ih, W_hh, b_ih, b_hh):
        import jax, jax.numpy as jnp
        import numpy as np
        N_NODES = 3125
        N_EDGES = 50000
        HIDDEN = 128
        N_ETYPES = 4
        N_STEPS = 4

        def _gru_cell(x, h, W_ih, W_hh, b_ih, b_hh):
            gi = x @ W_ih.T + b_ih
            gh = h @ W_hh.T + b_hh
            ir, iz, inn = jnp.split(gi, 3, axis=1)
            hr, hz, hn = jnp.split(gh, 3, axis=1)
            r = jax.nn.sigmoid(ir + hr)
            z = jax.nn.sigmoid(iz + hz)
            n = jnp.tanh(inn + r * hn)
            return (1.0 - z) * n + z * h
        etypes = jnp.argmax(edge_feat, axis=1)
        src, dst = (edge_index[0], edge_index[1])
        N = node_feat.shape[0]
        h = node_feat
        for _ in range(N_STEPS):
            trans = jnp.einsum('nd,tod->tno', h, W_edge) + b_edge[:, None, :]
            msg = trans[etypes, src]
            a = jax.ops.segment_sum(msg, dst, num_segments=N)
            h = _gru_cell(a, h, W_ih, W_hh, b_ih, b_hh)
        return h

    def _L1_gnn_ref(x, edge_index, edge_weights, W, a):
        import jax, jax.numpy as jnp
        import numpy as np
        N_NODES = 50000
        N_EDGES = 25000
        IN_F = 128
        OUT_F = 32
        HEADS = 4
        NEG_SLOPE = 0.2
        EPS = 1e-16
        num_nodes = x.shape[0]
        src, tgt = (edge_index[0], edge_index[1])
        h = jnp.einsum('nf,hfo->nho', x, W)
        a_src, a_tgt = (a[:, :OUT_F], a[:, OUT_F:])
        e_src = jnp.einsum('nho,ho->nh', h, a_src)
        e_tgt = jnp.einsum('nho,ho->nh', h, a_tgt)
        e = jax.nn.leaky_relu(e_src[src] + e_tgt[tgt], NEG_SLOPE)
        e = e * edge_weights[:, None]
        m = jax.ops.segment_max(e, tgt, num_segments=num_nodes)
        exp_e = jnp.exp(e - m[tgt])
        denom = jax.ops.segment_sum(exp_e, tgt, num_segments=num_nodes)
        att = exp_e / (denom[tgt] + EPS)
        weighted = h[src] * att[:, :, None]
        agg = jax.ops.segment_sum(weighted, tgt, num_segments=num_nodes)
        return agg.reshape(num_nodes, HEADS * OUT_F)
    edge_index = jnp.stack([src, dst])
    h = jnp.maximum(_layernorm(x, axis=-1), 0.0)
    x = x + _L0_gnn_ref(h, edge_index, edge_attr_4, L0_gnn_W_edge, L0_gnn_b_edge, L0_gnn_W_ih, L0_gnn_W_hh, L0_gnn_b_ih, L0_gnn_b_hh)
    h = jnp.maximum(_layernorm(x, axis=-1), 0.0)
    x = x + _L1_gnn_ref(h, edge_index, edge_weight, L1_gnn_W, L1_gnn_a)
    return x

_drawn_inputs = setup_inputs


def setup_inputs(seed=0):
    import zlib

    import numpy as np

    out = dict(_drawn_inputs(seed))
    spreads = {}
    factors = {'edge_weight': 3.974, 'L1_gnn_a': 3.433}
    for name, (base, spread) in spreads.items():
        noise = np.random.default_rng([zlib.crc32(name.encode()), seed]).standard_normal(out[name].shape)
        drawn = base * np.exp(spread * noise) if base else spread * noise
        out[name] = jnp.asarray(drawn.astype(out[name].dtype))
    for name, factor in factors.items():
        out[name] = (out[name] * factor).astype(out[name].dtype)
    return out
```

```python
from contextlib import ExitStack

import concourse.bass as bass
from concourse import mybir

fp32 = mybir.dt.float32
bf16 = mybir.dt.bfloat16
i32 = mybir.dt.int32
ALU = mybir.AluOpType
ACT = mybir.ActivationFunctionType
AX = mybir.AxisListType

P = 128
N, E, D = 3125, 50000, 128
TYPES, STEPS = 4, 4
HEADS, OUT_F = 4, 32
SLOPE, LN_EPS, DEN_EPS = 0.2, 1e-5, 1e-16
WIN, BLK = 64, 32
BANK = 512
OWN = BANK - WIN
CHUNKS = -(-N // OWN)
NP = CHUNKS * OWN
NT = -(-NP // P)
ROWS = [min(P, NP - P * t) for t in range(NT)]
NBLK = NP // BLK
NWIN = NP // WIN
NG, HALF = 14, 14
G = 2 * HALF
TILES = NG * G
QT = HALF // 2
PAIRS = HALF // 2
BATCHES = (range(0, 4), range(4, PAIRS))
R1 = D + HEADS
BIG = 2.0 ** 100
REGS = 16
NQ = TILES // 4
assert NG * G >= -(-E // P) and NQ <= P and NP >= N


class Order:

    def __init__(self, eng, sem):
        self.eng, self.sem, self.n, self.loops = eng, sem, 0, 0

    def mark(self, ins):
        ins.then_inc(self.sem, 1)
        self.n += 1

    def wait(self):
        self.eng.wait_ge(self.sem, self.loops + self.n)

    def link(self, ins):
        self.mark(ins)
        self.wait()

    def enter(self, i, per):
        was = (self.loops, self.n, per)
        self.loops = self.loops + i * per
        return was

    def leave(self, was, count):
        loops, n, per = was
        assert self.n - n == per, (self.n - n, per)
        self.loops, self.n = loops, n + per * count


def gnn_kernel(nc, x, src_t, dst_t, dst_rows, attr_t, ew_t, we_t, be, wih_t, whh_t, bih, bhh, w1, a1, out,
               force_rounds=None):
    ctx = ExitStack()
    with ctx:
        def sb(name, shape, dt=fp32):
            return ctx.enter_context(nc.sbuf_tensor(name, shape, dt))

        def sem(name):
            return ctx.enter_context(nc.semaphore(name))

        tab0 = nc.dram_tensor("tab0", (NP * TYPES, D), fp32, kind="Internal").ap()
        tab1 = nc.dram_tensor("tab1", (NP, R1), fp32, kind="Internal").ap()
        tab_s = nc.dram_tensor("tab_s", (NP, HEADS), fp32, kind="Internal").ap()
        tab_t = nc.dram_tensor("tab_t", (NP, HEADS), fp32, kind="Internal").ap()

        src_i = sb("src_i", [P, TILES], i32)
        dst_i = sb("dst_i", [P, TILES], i32)
        rows_i = sb("rows_i", [NQ, 4, P], i32)
        attr = sb("attr", [P, TILES, TYPES])
        ew = sb("ew", [P, TILES])
        src_f = sb("src_f", [P, TILES])
        dst_f = sb("dst_f", [P, TILES])
        rel = sb("rel", [P, TILES])
        idx0 = sb("idx0", [P, TILES], i32)
        etype = sb("etype", [P, TILES])
        tmp_e = sb("tmp_e", [P, TILES])
        rows_f = sb("rows_f", [NQ, 4, P])
        dmin = sb("dmin", [NQ, 4])
        dmax = sb("dmax", [NQ, 4])
        win_i = sb("win_i", [NQ, 4], i32)
        win_f = sb("win_f", [NQ, 4])
        over = sb("over", [NQ, 5])
        blk_f = sb("blk_f", [P, TILES])
        col_f = sb("col_f", [1, TILES])
        col_tab = sb("col_tab", [1, 2 * NG, REGS], i32)
        look_tab = sb("look_tab", [1, 2 * NG, REGS], i32)
        acc_tab = sb("acc_tab", [1, 2 * NG, REGS], i32)
        narrow_f = sb("narrow_f", [1, 2])
        narrow = sb("narrow", [1, 1], i32)
        ident = sb("ident", [P, P])
        ident4 = sb("ident4", [P, 4, P], bf16)
        iota_i = sb("iota_i", [P, WIN], i32)
        iota = sb("iota", [P, WIN])
        start_i = sb("start_i", [P, NWIN], i32)
        start_f = sb("start_f", [P, NWIN])
        start_col = sb("start_col", [1, NWIN], i32)
        zeros = sb("zeros", [P, BANK], bf16)
        eps = sb("eps", [P, 1])
        neg_big = sb("neg_big", [P, 1])
        xs = sb("xs", [P, NT, D])
        nrm = sb("nrm", [P, NT, D])
        stats = sb("stats", [P, NT, 6])
        mv = sb("mv", [P, NT, 2])
        rstd = sb("rstd", [P, NT])
        h_t = sb("h_t", [P, NP])
        agg_t = sb("agg_t", [P, NP])
        spill = sb("spill", [P, CHUNKS, WIN])
        gh = sb("gh", [P, 3, NP])
        over_gh = gh[:, :, :].rearrange("p g n -> p (g n)")
        n_pick, n_wmsg, n_hot_t = PAIRS * HEADS * P, G * D, PAIRS * P
        pick = over_gh[0:HALF * HEADS, 0:n_pick].rearrange("p (j f b n) -> p j f b n", j=PAIRS, f=HEADS, b=2)
        wmsg = over_gh[:, n_pick:n_pick + n_wmsg].rearrange("p (k d) -> p k d", d=D)
        hot_t = over_gh[:, n_pick + n_wmsg:n_pick + n_wmsg + n_hot_t].rearrange("p (j e) -> p j e", e=P)
        rz = sb("rz", [P, 3, 2, OWN])
        cand = sb("cand", [P, 2, OWN])
        dlt = sb("dlt", [P, OWN])
        we_s = sb("we_s", [P, TYPES * D])
        be_s = sb("be_s", [P, TYPES * D])
        wih_s = sb("wih_s", [P, 3 * D])
        whh_s = sb("whh_s", [P, 3 * D])
        bih_s = sb("bih_s", [P, 3])
        bhh_s = sb("bhh_s", [P, 3])
        bgh = sb("bgh", [P, 3])
        w1_s = sb("w1_s", [P, D + 2 * HEADS])
        a_s = sb("a_s", [P, 2, HEADS, OUT_F])
        wa = sb("wa", [P, 2, HEADS, OUT_F])
        stage = [sb(f"stage{h}", [P, HALF], i32) for h in range(2)]
        msg = sb("msg", [P, G, R1])
        srow = sb("srow", [P, G, HEADS])
        hot = sb("hot", [P, G, WIN])
        neg = sb("neg", [P, G, WIN], bf16)
        rel_w = sb("rel_w", [P, G])
        tabst = sb("tabst", [P, 3, TYPES * D])
        scr = sb("scr", [P, HALF, HEADS])
        lgt = sb("lgt", [P, HALF, HEADS])
        ex = sb("ex", [P, HALF, HEADS])
        lgt_t = sb("lgt_t", [HALF * HEADS, P])
        pmax = sb("pmax", [P, 2, HEADS])
        m_acc = sb("m_acc", [P, NBLK * HEADS])
        d_acc = sb("d_acc", [P, NBLK * HEADS])
        look_a = sb("look_a", [P, NBLK, 2 * HEADS])
        look_b = sb("look_b", [P, NBLK, 2 * HEADS])
        t32 = sb("t32", [BLK, NBLK, HEADS])
        sh = sb("sh", [BLK, 3, NBLK, HEADS])
        den = sb("den", [P, NT, HEADS])

        ps = ctx.enter_context(nc.psum_tensor("ps", [P, 8, BANK], fp32))
        acc = ps[:, :, :].rearrange("p b c -> p (b c)")

        s_ld_e, s_ld_x, s_ld_w = sem("s_ld_e"), sem("s_ld_x"), sem("s_ld_w")
        s_pool = sem("s_pool")
        s_const = sem("s_const")
        s_dve = sem("s_dve")
        s_win, s_winb, s_flag = sem("s_win"), sem("s_winb"), sem("s_flag")
        s_xt, s_var, s_sd, s_nrm, s_nt, s_relu = (sem(f"s_{n}") for n in ("xt", "var", "sd", "nrm", "nt", "relu"))
        s_xadd = sem("s_xadd")
        s_h = sem("s_h")
        s_tp, s_tf = sem("s_tp"), sem("s_tf")
        s_tw = [sem(f"s_tw{i}") for i in range(3)]
        s_gh, s_ghf = sem("s_gh"), sem("s_ghf")
        s_arr = [sem(f"s_arr{q}") for q in range(4)]
        s_idx = [sem(f"s_idx{h}") for h in range(2)]
        s_hot = [sem(f"s_hot{h}") for h in range(2)]
        s_used = [sem(f"s_used{h}") for h in range(2)]
        s_sum, s_ev, s_agg = sem("s_sum"), sem("s_ev"), sem("s_agg")
        s_gi, s_pre, s_sig, s_npre, s_tanh = (sem(f"s_{n}") for n in ("gi", "pre", "sig", "npre", "tanh"))
        s_lp, s_lf = sem("s_lp"), sem("s_lf")
        s_lw = [sem(f"s_lw{i}") for i in range(3)]
        s_t32, s_look, s_mx = sem("s_t32"), sem("s_look"), sem("s_mx")
        s_neg, s_otp, s_ot, s_lk = sem("s_neg"), sem("s_otp"), sem("s_ot"), sem("s_lk")
        s_lgt, s_ltp, s_lt, s_bc, s_bcf = sem("s_lgt"), sem("s_ltp"), sem("s_lt"), sem("s_bc"), sem("s_bcf")
        s_shift, s_ex, s_wm, s_den, s_denf = sem("s_shift"), sem("s_ex"), sem("s_wm"), sem("s_den"), sem("s_denf")
        s_fin, s_out, s_w = sem("s_fin"), sem("s_out"), sem("s_w")

        block = ctx.enter_context(nc.Block())

        def chunk_of(t):
            return (P * t + ROWS[t] - 1) // OWN

        def rounds_loop(eng, rounds, body):
            if rounds == 1:
                body(0)
            else:
                with eng.Fori(0, rounds, 1) as w:
                    body(w)

        def places(eng, table, g, h, top):
            loaded = nc.values_load_multi_w_load_instructions(
                table[0:1, bass.ds(g * 2 + h, 1), :].rearrange("p a b -> p (a b)"), engines=[eng.engine],
                min_val=0, max_val=top)[1]
            return loaded[0:HALF]

        def either(eng, program, order=None):
            eng.wait_ge(s_flag, 1)
            before = order.n if order else 0
            if force_rounds:
                return program(force_rounds)
            flag = eng.value_load(narrow[0:1, 0:1], min_val=0, max_val=1)
            with eng.If(flag):
                program(1)
            with eng.Else():
                if order:
                    order.n = before
                program(NWIN)

        tab_uses = [len(range(i, NT, 3)) for i in range(3)]

        @block.sync
        def _(sp):
            sp.dma_start(rows_i[:], dst_rows).then_inc(s_ld_e, 16)
            sp.dma_start(src_i[:], src_t).then_inc(s_ld_e, 16)
            sp.dma_start(dst_i[:], dst_t).then_inc(s_ld_e, 16)
            sp.dma_start(attr[:], attr_t).then_inc(s_ld_e, 16)
            sp.dma_start(ew[:], ew_t).then_inc(s_ld_e, 16)
            sp.wait_ge(s_const, 1)
            full = N // P
            sp.dma_start(xs[:, 0:full, :], x[0:full * P, :].rearrange("(t p) d -> p t d", p=P)).then_inc(s_ld_x, 16)
            sp.dma_start(xs[0:N - full * P, full, :], x[full * P:N, :]).then_inc(s_ld_x, 16)
            for dst, src in ((we_s[:], we_t), (be_s[:], be.partition_broadcast(P)), (wih_s[:], wih_t),
                             (whh_s[:], whh_t), (bih_s[:], bih), (bhh_s[:], bhh),
                             (w1_s[:, 0:D], w1), (a_s[:], a1.partition_broadcast(P))):
                sp.dma_start(dst, src).then_inc(s_ld_w, 16)
            with nc.sync.Fori(0, STEPS, 1) as st:
                for t in range(NT):
                    sp.wait_ge(s_tf, st * NT + t + 1)
                    sp.dma_start(tab0[TYPES * P * t:TYPES * (P * t + ROWS[t]), :].rearrange("(p k) d -> p (k d)", k=TYPES),
                                 tabst[0:ROWS[t], t % 3, :]).then_inc(s_tw[t % 3], 16)
            for t in range(NT):
                sp.wait_ge(s_lf, t + 1)
                r, s = ROWS[t], slice(P * t, P * t + ROWS[t])
                sp.dma_start(tab1[s, :], tabst[0:r, t % 3, 0:R1]).then_inc(s_lw[t % 3], 16)
                sp.dma_start(tab_s[s, :], tabst[0:r, t % 3, D:R1]).then_inc(s_lw[t % 3], 16)
                sp.dma_start(tab_t[s, :], tabst[0:r, t % 3, R1:R1 + HEADS]).then_inc(s_lw[t % 3], 16)
            for i in range(3):
                sp.wait_ge(s_lw[i], 48 * tab_uses[i])
            sp.dma_start(t32[:], tab_t.rearrange("(c p) h -> p c h", p=BLK)).then_inc(s_t32, 16)
            sp.wait_ge(s_fin, NT - 1)
            sp.dma_start(out[0:full * P, :].rearrange("(t p) d -> p t d", p=P), nrm[:, 0:full, :]).then_inc(s_out, 16)
            sp.wait_ge(s_fin, NT)
            sp.dma_start(out[full * P:N, :], nrm[0:N - full * P, full, :]).then_inc(s_out, 16)
            sp.wait_ge(s_out, 32)

        @block.gpsimd
        def _(pool):
            pool.iota(iota_i[:], pattern=[[1, WIN]], base=0, channel_multiplier=0).then_inc(s_pool, 1)
            pool.iota(start_i[:], pattern=[[WIN, NWIN]], base=0, channel_multiplier=0).then_inc(s_pool, 1)
            pool.iota(start_col[:], pattern=[[BANK, CHUNKS], [WIN, OWN // WIN]], base=0,
                      channel_multiplier=0).then_inc(s_pool, 1)
            pool.memset(ident[:], 0.0).then_inc(s_pool, 1)
            pool.wait_ge(s_pool, 4)
            pool.affine_select(out=ident[:], in_=ident[:], compare_op=ALU.not_equal, fill=1.0, base=0,
                               pattern=[[-1, P]], channel_multiplier=1).then_inc(s_pool, 1)

            def wait_on(sem, value):
                value = pool.snap(value)
                pool.keepalive_nop([pool.lower_val_access(value)])
                pool.wait_ge(s_pool, 5)
                pool.wait_ge(sem, value)

            def gathers(n, table, to):
                for h in range(2):
                    wait_on(s_idx[h], n + 1)
                    for k in range(HALF):
                        slot = h * HALF + k
                        pool.indirect_dma_start(to[:, slot, :], None, table,
                                                bass.IndirectOffsetOnAxis(stage[h][:, k:k + 1], 0)
                                                ).then_inc(s_arr[slot // QT], 16)

            with nc.gpsimd.Fori(0, STEPS, 1) as st:
                for i in range(3):
                    wait_on(s_tw[i], (st + 1) * (16 * tab_uses[i]))
                with nc.gpsimd.Fori(0, NG, 1) as g:
                    gathers(st * NG + g, tab0, msg[:, :, 0:D])
            for i in range(3):
                pool.wait_ge(s_lw[i], 48 * tab_uses[i])
            with nc.gpsimd.Fori(0, NG, 1) as g:
                gathers(g + STEPS * NG, tab_s, srow)
            with nc.gpsimd.Fori(0, NG, 1) as g:
                gathers(g + (STEPS + 1) * NG, tab1, msg)

        @block.scalar
        def _(act):
            def norm(n):
                act.wait_ge(s_var, n + 1)
                act.activation(rstd[:], mv[:, :, 1], ACT.Sqrt, bias=eps[:, 0:1]).then_inc(s_sd, 1)
                for t in range(NT):
                    act.wait_ge(s_nt, n * NT + t + 1)
                    act.activation(h_t[:, P * t:P * t + ROWS[t]], ps[:, 4 + t % 4, 0:ROWS[t]],
                                   ACT.Relu).then_inc(s_relu, 1)

            def sum_out(st):
                for c in range(CHUNKS):
                    act.wait_ge(s_sum, st * CHUNKS + c + 1)
                    act.activation(agg_t[:, OWN * c:OWN * (c + 1)], ps[:, c, 0:OWN], ACT.Copy)
                    act.activation(spill[:, c, :], ps[:, c, OWN:BANK], ACT.Copy).then_inc(s_ev, 1)

            def program(rounds):
                with nc.scalar.Fori(0, STEPS, 1) as st:
                    for m in range(3 * CHUNKS):
                        g, c = m % 3, m // 3
                        act.wait_ge(s_gh, st * (3 * CHUNKS) + m + 1)
                        act.activation(gh[:, g, OWN * c:OWN * (c + 1)], ps[:, m % 6, 0:OWN], ACT.Identity,
                                       bias=bgh[:, g:g + 1]).then_inc(s_ghf, 1)
                    sum_out(st)
                    for i in range(CHUNKS + 1):
                        if i < CHUNKS:
                            act.wait_ge(s_pre, st * CHUNKS + i + 1)
                            act.activation(rz[:, i % 3, :, :], rz[:, i % 3, :, :], ACT.Sigmoid).then_inc(s_sig, 1)
                        if i >= 1:
                            act.wait_ge(s_npre, st * CHUNKS + i)
                            act.activation(cand[:, (i - 1) % 2, :], cand[:, (i - 1) % 2, :], ACT.Tanh,
                                           bias=bih_s[:, 2:3]).then_inc(s_tanh, 1)
                norm(1)
                for t in range(NT):
                    act.wait_ge(s_lp, t + 1)
                    if t >= 3:
                        act.wait_ge(s_lw[t % 3], 48 * (t // 3))
                    act.activation(tabst[0:ROWS[t], t % 3, 0:R1 + HEADS], ps[0:ROWS[t], t % 2, 0:R1 + HEADS],
                                   ACT.Copy).then_inc(s_lf, 1)

                def max_half(g, h):
                    def one(w):
                        n = (g * 2 + h) * rounds + w
                        act.wait_ge(s_hot[h], (g + STEPS * NG) * rounds + w + 1)
                        if True:
                            act.activation(neg[:, h * HALF:(h + 1) * HALF, :], hot[:, h * HALF:(h + 1) * HALF, :],
                                           ACT.Identity, scale=BIG, bias=neg_big[:, 0:1]).then_inc(s_neg, 1)
                        act.wait_ge(s_otp, n + 1)
                        act.activation(hot_t[:, 0:4, :], ps[:, 0, :].rearrange("p (j e) -> p j e", e=P), ACT.Copy)
                        act.activation(hot_t[:, 4:7, :], ps[:, 1, 0:3 * P].rearrange("p (j e) -> p j e", e=P),
                                       ACT.Copy).then_inc(s_ot, 1)
                        act.wait_ge(s_ltp, n + 1)
                        act.activation(lgt_t[:], ps[0:HALF * HEADS, 3, 0:P], ACT.Copy).then_inc(s_lt, 1)
                    rounds_loop(nc.scalar, rounds, one)

                with nc.scalar.Fori(0, NG, 1) as g:
                    for h in range(2):
                        max_half(g, h)

                def sum_half(g, h):
                    def one(w):
                        n = (g * 2 + h) * rounds + w
                        for b, js in enumerate(BATCHES):
                            act.wait_ge(s_otp, (2 * NG * rounds) + n * len(BATCHES) + b + 1)
                            act.activation(hot_t[:, js.start:js.stop, :],
                                           ps[:, 7, 0:P * len(js)].rearrange("p (j e) -> p j e", e=P),
                                           ACT.Copy).then_inc(s_ot, 1)
                        act.wait_ge(s_shift, n + 1)
                        act.activation(ex[:], lgt[:], ACT.Exp).then_inc(s_ex, 1)
                    rounds_loop(nc.scalar, rounds, one)

                with nc.scalar.Fori(0, NG, 1) as g:
                    for h in range(2):
                        sum_half(g, h)
                sum_out(STEPS)

            act.wait_ge(s_const, 2)
            norm(0)
            either(act, program)

        @block.tensor
        def _(pe):
            mm = nc.tensor.matmul

            def norm(n):
                if n:
                    pe.wait_ge(s_npre, CHUNKS * STEPS)
                    for t in range(NT):
                        pe.wait_ge(s_h, CHUNKS * STEPS + chunk_of(t) + 1)
                        if t >= 4:
                            pe.wait_ge(s_xadd, t - 3)
                        nc.tensor.transpose(ps[0:ROWS[t], t % 4, 0:P], h_t[:, P * t:P * t + ROWS[t]],
                                            ident[:]).then_inc(s_xt, 1)
                for t in range(NT):
                    pe.wait_ge(s_nrm, n * NT + t + 1)
                    if t >= 4:
                        pe.wait_ge(s_relu, n * NT + t - 3)
                    nc.tensor.transpose(ps[:, 4 + t % 4, 0:ROWS[t]], nrm[0:ROWS[t], t, :],
                                        ident[0:ROWS[t], 0:ROWS[t]]).then_inc(s_nt, 1)

            def open_sums():
                for c in range(CHUNKS):
                    mm(ps[:, c, :], zeros[:, 0:P], zeros[:], start=True, stop=False)

            def close_sums():
                for c in range(CHUNKS):
                    mm(ps[:, c, :], zeros[:, 0:P], zeros[:], start=False, stop=True).then_inc(s_sum, 1)

            def program(rounds):
                def columns(g, h, w):
                    top = CHUNKS * BANK - WIN
                    if rounds == 1:
                        return places(pe, col_tab, g, h, top)
                    return [pe.value_load(start_col[0:1, bass.ds(w, 1)], min_val=0, max_val=top)] * HALF

                def look_places(g, h, w):
                    if rounds == 1:
                        return places(pe, look_tab, g, h, 2 * HEADS * (NBLK - 1))
                    return [w * (4 * HEADS)] * HALF

                def add_half(n, g, h):
                    def one(w):
                        for q in (2 * h, 2 * h + 1):
                            pe.wait_ge(s_arr[q], (n + 1) * (16 * QT))
                        pe.wait_ge(s_hot[h], n * rounds + w + 1)
                        cols = columns(g, h, w)
                        for k in range(HALF):
                            slot = h * HALF + k
                            last = mm(acc[:, bass.ds(cols[k], WIN)], msg[:, slot, 0:D], hot[:, slot, :], start=False, stop=False)
                        last.then_inc(s_used[h], 1)
                    rounds_loop(nc.tensor, rounds, one)

                with nc.tensor.Fori(0, STEPS, 1) as st:
                    for t in range(NT):
                        pe.wait_ge(s_h, st * CHUNKS + chunk_of(t) + 1)
                        if t >= 2:
                            pe.wait_ge(s_tf, st * NT + t - 1)
                        mm(ps[0:ROWS[t], 6 + t % 2, :], h_t[:, P * t:P * t + ROWS[t]], we_s[:],
                           start=True, stop=True).then_inc(s_tp, 1)
                    for m in range(3 * CHUNKS):
                        g, c = m % 3, m // 3
                        if m >= 6:
                            pe.wait_ge(s_ghf, st * (3 * CHUNKS) + m - 5)
                        mm(ps[:, m % 6, 0:OWN], whh_s[:, D * g:D * (g + 1)], h_t[:, OWN * c:OWN * (c + 1)],
                           start=True, stop=True).then_inc(s_gh, 1)
                    pe.wait_ge(s_ghf, (st + 1) * (3 * CHUNKS))
                    pe.wait_ge(s_tf, (st + 1) * NT)
                    open_sums()
                    with nc.tensor.Fori(0, NG, 1) as g:
                        for h in range(2):
                            add_half(st * NG + g, g, h)
                    close_sums()
                    pe.wait_ge(s_ev, (st + 1) * CHUNKS)
                    for c in range(CHUNKS):
                        if c >= 1:
                            pe.wait_ge(s_agg, st * (CHUNKS - 1) + c)
                        if c >= 2:
                            pe.wait_ge(s_npre, st * CHUNKS + c - 1)
                        for g in range(3):
                            last = mm(ps[:, 3 * (c % 2) + g, 0:OWN], wih_s[:, D * g:D * (g + 1)],
                                      agg_t[:, OWN * c:OWN * (c + 1)], start=True, stop=True)
                        last.then_inc(s_gi, 1)
                norm(1)
                for t in range(NT):
                    pe.wait_ge(s_relu, NT + t + 1)
                    if t >= 2:
                        pe.wait_ge(s_lf, t - 1)
                    mm(ps[0:ROWS[t], t % 2, 0:R1 + HEADS], h_t[:, P * t:P * t + ROWS[t]], w1_s[:],
                       start=True, stop=True).then_inc(s_lp, 1)
                pe.wait_ge(s_lf, NT)

                def lookups(where, cols, at):
                    for k in range(HALF):
                        flat = (look_a, look_b)[k % 2][:, :, :].rearrange("p c f -> p (c f)")
                        last = mm(at[:, k * cols:(k + 1) * cols], hot_t[:, k // 2, :],
                                  flat[:, bass.ds(where[k], cols)], start=True, stop=True)
                    return last

                pe.wait_ge(s_look, 1)

                def max_half(g, h):
                    def one(w):
                        n = (g * 2 + h) * rounds + w
                        pe.wait_ge(s_hot[h], (g + STEPS * NG) * rounds + w + 1)
                        for j in range(PAIRS):
                            s0 = h * HALF + 2 * j
                            last = nc.tensor.transpose(ps[:, j // 4, P * (j % 4):P * (j % 4 + 1)],
                                                       hot[:, s0:s0 + 2, :].rearrange("p a b -> p (a b)"), ident[:])
                        last.then_inc(s_otp, 1)
                        pe.wait_ge(s_ot, n + 1)
                        lookups(look_places(g, h, w), HEADS, ps[:, 2, :]).then_inc(s_lk, 1)
                        have = pe.snap(n + 1)
                        pe.wait_ge(s_look, 1)
                        pe.wait_ge(s_lgt, have)
                        nc.tensor.transpose(ps[0:HALF * HEADS, 3, 0:P], lgt[:].rearrange("p a b -> p (a b)"),
                                            ident[:]).then_inc(s_ltp, 1)
                        pe.wait_ge(s_neg, n + 1)
                        pe.wait_ge(s_lt, n + 1)
                        for j in range(PAIRS):
                            bank = ps[:, 4 + j % 4, :]
                            if j >= 4:
                                pe.wait_ge(s_bcf, n * PAIRS + j - 3)
                            s0 = h * HALF + 2 * j
                            mm(bank, neg[:, s0:s0 + 2, :].rearrange("p a b -> p (a b)"),
                               ident4[:].rearrange("p a b -> p (a b)"), start=True, stop=False)
                            for hd in range(HEADS):
                                last = mm(bank[:, P * hd:P * (hd + 1)], pick[:, j, hd, :, :].rearrange("p a b -> p (a b)"), lgt_t[:], start=False, stop=(hd == HEADS - 1))
                            last.then_inc(s_bc, 1)
                        pe.wait_ge(s_bcf, (n + 1) * PAIRS)
                        mm(ps[:, 2, 0:4], zeros[:, 0:P], zeros[:, 0:4], start=True, stop=True).then_inc(s_used[h], 1)
                    rounds_loop(nc.tensor, rounds, one)

                with nc.tensor.Fori(0, NG, 1) as g:
                    for h in range(2):
                        max_half(g, h)
                pe.wait_ge(s_mx, 1)
                open_sums()
                look_ps = ps[:, 7, 0:HALF * 2 * HEADS]
                den_ps = ps[:, 7, HALF * 2 * HEADS:HALF * 2 * HEADS + PAIRS * HEADS]

                def sum_half(g, h):
                    def one(w):
                        for q in (2 * h, 2 * h + 1):
                            pe.wait_ge(s_arr[q], (g + (STEPS + 1) * NG + 1) * (16 * QT))
                        n = (g * 2 + h) * rounds + w
                        pe.wait_ge(s_hot[h], (g + (STEPS + 1) * NG) * rounds + w + 1)
                        for b, js in enumerate(BATCHES):
                            for i, j in enumerate(js):
                                s0 = h * HALF + 2 * j
                                last = nc.tensor.transpose(ps[:, 7, P * i:P * (i + 1)],
                                                           hot[:, s0:s0 + 2, :].rearrange("p a b -> p (a b)"), ident[:])
                            last.then_inc(s_otp, 1)
                            pe.wait_ge(s_ot, 2 * NG * rounds + n * len(BATCHES) + b + 1)
                        lookups(look_places(g, h, w), 2 * HEADS, look_ps).then_inc(s_lk, 1)
                        pe.wait_ge(s_ex, n + 1)
                        for k in range(HALF):
                            slot = h * HALF + k
                            lo = WIN * (k % 2)
                            last = mm(den_ps[lo:lo + WIN, HEADS * (k // 2):HEADS * (k // 2 + 1)], hot[:, slot, :], ex[:, k, :],
                                      start=True, stop=True)
                        last.then_inc(s_den, 1)
                        pe.wait_ge(s_wm, n + 1)
                        cols = columns(g, h, w)
                        for k in range(HALF):
                            slot = h * HALF + k
                            last = mm(acc[:, bass.ds(cols[k], WIN)], wmsg[:, slot, :], hot[:, slot, :], start=False, stop=False)
                        last.then_inc(s_used[h], 1)
                    rounds_loop(nc.tensor, rounds, one)

                with nc.tensor.Fori(0, NG, 1) as g:
                    for h in range(2):
                        sum_half(g, h)
                close_sums()
                pe.wait_ge(s_ev, (STEPS + 1) * CHUNKS)
                for t in range(NT):
                    c = chunk_of(t)
                    if c >= 1:
                        pe.wait_ge(s_agg, STEPS * (CHUNKS - 1) + c)
                    if t >= 4:
                        pe.wait_ge(s_fin, t - 3)
                    nc.tensor.transpose(ps[0:ROWS[t], t % 4, 0:P], agg_t[:, P * t:P * t + ROWS[t]],
                                        ident[:]).then_inc(s_xt, 1)

            pe.wait_ge(s_pool, 5)
            pe.wait_ge(s_const, 2)
            pe.wait_ge(s_win, 1)
            for q in range(4):
                last = mm(ps[:, 0, NQ * q:NQ * (q + 1)], win_f[:, q:q + 1].to_broadcast([NQ, P]),
                          ident[0:NQ, 0:NQ], start=True, stop=True)
            last.then_inc(s_winb, 1)
            nc.tensor.transpose(ps[0:1, 1, 0:NQ], over[:, 4:5], ident[0:NQ, 0:NQ]).then_inc(s_winb, 1)
            norm(0)
            either(pe, program)

        @block.vector
        def _(dve):
            order = Order(dve, s_dve)
            link, mark = order.link, order.mark
            tt, ts, stt, cp = nc.vector.tensor_tensor, nc.vector.tensor_scalar, nc.vector.scalar_tensor_tensor, nc.vector.tensor_copy

            def norm(n):
                for t in range(NT):
                    if n:
                        dve.wait_ge(s_xt, t + 1)
                        tt(xs[0:ROWS[t], t, :], xs[0:ROWS[t], t, :], ps[0:ROWS[t], t % 4, 0:P], ALU.add).then_inc(s_xadd, 1)
                        dve.wait_ge(s_xadd, t + 1)
                    nc.vector.bn_stats(stats[:, t, :], xs[:, t, :]).then_inc(s_dve, 1)
                    order.n += 1
                order.wait()
                for t in range(NT):
                    last = nc.vector.bn_aggr(mv[:, t, :], stats[:, t, :])
                last.then_inc(s_var, 1)
                dve.wait_ge(s_sd, n + 1)
                link(nc.vector.reciprocal(rstd[:], rstd[:]))
                for t in range(NT):
                    ts(nrm[:, t, :], xs[:, t, :], mv[:, t, 0:1], rstd[:, t:t + 1], ALU.subtract, ALU.mult).then_inc(s_nrm, 1)

            def overlaps(st):
                dve.wait_ge(s_ev, (st + 1) * CHUNKS)
                for c in range(1, CHUNKS):
                    tt(agg_t[:, OWN * c:OWN * c + WIN], agg_t[:, OWN * c:OWN * c + WIN], spill[:, c - 1, :],
                       ALU.add).then_inc(s_agg, 1)

            def program(rounds):
                def acc_places(g, h, w):
                    if rounds == 1:
                        return places(dve, acc_tab, g, h, HEADS * (NBLK - 1))
                    return [w * (2 * HEADS)] * HALF

                def free_half(n, h, w):
                    dve.wait_ge(s_used[h], n * rounds + w + 1)

                def build_hot(n, g, h, w):
                    sl = slice(h * HALF, (h + 1) * HALF)
                    if rounds == 1:
                        r = rel[:, bass.ds(g * G + h * HALF, HALF)]
                    else:
                        link(ts(rel_w[:, sl], dst_f[:, bass.ds(g * G + h * HALF, HALF)], start_f[:, bass.ds(w, 1)], None,
                                ALU.subtract))
                        r = rel_w[:, sl]
                    tt(hot[:, sl, :], iota[:].unsqueeze(1).to_broadcast([P, HALF, WIN]),
                       r.unsqueeze(2).to_broadcast([P, HALF, WIN]), ALU.is_equal).then_inc(s_hot[h], 1)

                def stage_idx(n, g, h, idx):
                    cp(stage[h][:], idx[:, bass.ds(g * G + h * HALF, HALF)]).then_inc(s_idx[h], 1)

                extra = 0 if rounds == 1 else 1

                with nc.vector.Fori(0, STEPS, 1) as st:
                    step = order.enter(st, extra * 2 * NG * rounds + 3 * CHUNKS)
                    for t in range(NT):
                        dve.wait_ge(s_tp, st * NT + t + 1)
                        if t >= 3:
                            dve.wait_ge(s_tw[t % 3], st * (16 * tab_uses[t % 3]) + 16 * (t // 3))
                        tt(tabst[0:ROWS[t], t % 3, :], ps[0:ROWS[t], 6 + t % 2, :], be_s[0:ROWS[t], :], ALU.add).then_inc(s_tf, 1)
                    with nc.vector.Fori(0, NG, 1) as g:
                        it = order.enter(g, extra * 2 * rounds)
                        for h in range(2):
                            n = st * NG + g
                            free_half(n, h, 0)
                            stage_idx(n, g, h, idx0)

                            def one(w):
                                was = order.enter(w, extra)
                                free_half(n, h, w)
                                build_hot(n, g, h, w)
                                order.leave(was, rounds)
                            rounds_loop(nc.vector, rounds, one)
                        order.leave(it, NG)
                    overlaps(st)
                    for i in range(CHUNKS + 2):
                        if i < CHUNKS:
                            c = i
                            dve.wait_ge(s_gi, st * CHUNKS + c + 1)
                            if c >= 3:
                                dve.wait_ge(s_h, (st + 1) * CHUNKS + c - 2)
                            for g in range(2):
                                last = tt(rz[:, c % 3, g, :], ps[:, 3 * (c % 2) + g, 0:OWN], gh[:, g, OWN * c:OWN * (c + 1)], ALU.add)
                            last.then_inc(s_pre, 1)
                        if 1 <= i <= CHUNKS:
                            c = i - 1
                            dve.wait_ge(s_sig, st * CHUNKS + c + 1)
                            if c >= 2:
                                dve.wait_ge(s_h, (st + 1) * CHUNKS + c - 1)
                            link(tt(cand[:, c % 2, :], rz[:, c % 3, 0, :], gh[:, 2, OWN * c:OWN * (c + 1)], ALU.mult))
                            tt(cand[:, c % 2, :], cand[:, c % 2, :], ps[:, 3 * (c % 2) + 2, 0:OWN], ALU.add).then_inc(s_npre, 1)
                        if i >= 2:
                            c = i - 2
                            own = slice(OWN * c, OWN * (c + 1))
                            dve.wait_ge(s_tanh, st * CHUNKS + c + 1)
                            if c >= 1:
                                dve.wait_ge(s_h, (st + 1) * CHUNKS + c)
                            link(tt(dlt[:], h_t[:, own], cand[:, c % 2, :], ALU.subtract))
                            link(tt(dlt[:], dlt[:], rz[:, c % 3, 1, :], ALU.mult))
                            tt(h_t[:, own], cand[:, c % 2, :], dlt[:], ALU.add).then_inc(s_h, 1)
                    order.leave(step, STEPS)
                norm(1)

                def place(at):
                    for table, p0 in ((look_a, 0), (look_b, 2 * BLK)):
                        cp(table[p0:p0 + BLK, :, at:at + HEADS], t32[:])
                        last = cp(table[p0 + BLK:p0 + 2 * BLK, 0:NBLK - 1, at:at + HEADS], t32[:, 1:NBLK, :])
                    return last

                def merge(table, op):
                    v = table[:].rearrange("p (c f) -> p c f", f=HEADS)
                    for q in range(3):
                        mark(cp(sh[:, q, :, :], v[BLK * (q + 1):BLK * (q + 2), :, :]))
                    order.wait()
                    link(tt(t32[:], v[0:BLK, :, :], sh[:, 1, :, :], op))
                    link(tt(t32[:, 1:, :], t32[:, 1:, :], sh[:, 0, 0:NBLK - 1, :], op))
                    link(tt(t32[:, 1:, :], t32[:, 1:, :], sh[:, 2, 0:NBLK - 1, :], op))

                rows_of = ident[0:HALF * HEADS, 0:HALF * HEADS].rearrange("p (j b f) -> p j b f", b=2, f=HEADS)
                for b in range(2):
                    for j in range(PAIRS):
                        last = cp(pick[:, j, :, b, :], rows_of[:, j, b, :].unsqueeze(2).to_broadcast([HALF * HEADS, HEADS, WIN]))
                mark(last)
                dve.wait_ge(s_t32, 16)
                place(0).then_inc(s_look, 1)

                def logits(h, scores, cols, look_ps):
                    link(tt(scr[:], look_ps.rearrange("p (k f) -> p k f", f=cols)[:, :, 0:HEADS], scores, ALU.add))
                    link(stt(lgt[:], scr[:], SLOPE, scr[:], ALU.mult, ALU.max))

                def weigh(g, h):
                    return tt(lgt[:], lgt[:], ew[:, bass.ds(g * G + h * HALF, HALF)].unsqueeze(2).to_broadcast([P, HALF, HEADS]), ALU.mult)

                def scatter(table, part, where, j, op):
                    for b in range(2):
                        lo = WIN * b
                        at = table[lo:lo + WIN, bass.ds(where[2 * j + b], HEADS)]
                        last = tt(at, at, part[lo:lo + WIN, :], op)
                    mark(last)
                    order.wait()

                def max_half(g, h):
                    n1 = g + STEPS * NG
                    free_half(n1, h, 0)
                    stage_idx(n1, g, h, src_i)

                    def one(w):
                        n = (g * 2 + h) * rounds + w
                        was = order.enter(w, extra + 2 + PAIRS)
                        free_half(n1, h, w)
                        build_hot(n1, g, h, w)
                        for q in (2 * h, 2 * h + 1):
                            dve.wait_ge(s_arr[q], (n1 + 1) * (16 * QT))
                        dve.wait_ge(s_lk, n + 1)
                        logits(h, srow[:, h * HALF:(h + 1) * HALF, :], HEADS, ps[:, 2, 0:HALF * HEADS])
                        weigh(g, h).then_inc(s_lgt, 1)
                        where = acc_places(g, h, w)
                        for j in range(PAIRS):
                            dve.wait_ge(s_bc, n * PAIRS + j + 1)
                            nc.vector.tensor_reduce(pmax[:, j % 2, :], ps[:, 4 + j % 4, :].rearrange("p (f e) -> p f e", e=P),
                                                    AX.X, ALU.max).then_inc(s_bcf, 1)
                            dve.wait_ge(s_bcf, n * PAIRS + j + 1)
                            scatter(m_acc, pmax[:, j % 2, :], where, j, ALU.max)
                        order.leave(was, rounds)
                    rounds_loop(nc.vector, rounds, one)

                with nc.vector.Fori(0, NG, 1) as g:
                    it = order.enter(g, 2 * rounds * (extra + 2 + PAIRS))
                    for h in range(2):
                        max_half(g, h)
                    order.leave(it, NG)
                merge(m_acc, ALU.max)
                place(HEADS).then_inc(s_mx, 1)

                look_ps = ps[:, 7, 0:HALF * 2 * HEADS]
                den_ps = ps[:, 7, HALF * 2 * HEADS:HALF * 2 * HEADS + PAIRS * HEADS]

                def sum_half(g, h):
                    n2 = g + (STEPS + 1) * NG
                    free_half(n2, h, 0)
                    stage_idx(n2, g, h, src_i)
                    sl = slice(h * HALF, (h + 1) * HALF)

                    def one(w):
                        n = (g * 2 + h) * rounds + w
                        was = order.enter(w, extra + 4 + PAIRS)
                        free_half(n2, h, w)
                        build_hot(n2, g, h, w)
                        for q in (2 * h, 2 * h + 1):
                            dve.wait_ge(s_arr[q], (n2 + 1) * (16 * QT))
                        dve.wait_ge(s_lk, 2 * NG * rounds + n + 1)
                        logits(h, msg[:, sl, D:R1], 2 * HEADS, look_ps)
                        link(weigh(g, h))
                        link(tt(lgt[:], lgt[:], look_ps.rearrange("p (k f) -> p k f", f=2 * HEADS)[:, :, HEADS:], ALU.subtract))
                        ts(lgt[:], lgt[:], 0.0, None, ALU.min).then_inc(s_shift, 1)
                        dve.wait_ge(s_ex, n + 1)
                        tt(wmsg[:, sl, :].rearrange("p k (f o) -> p k f o", o=OUT_F), msg[:, sl, 0:D].rearrange("p k (f o) -> p k f o", o=OUT_F),
                           ex[:].unsqueeze(3).to_broadcast([P, HALF, HEADS, OUT_F]), ALU.mult).then_inc(s_wm, 1)
                        where = acc_places(g, h, w)
                        dve.wait_ge(s_den, n + 1)
                        for j in range(PAIRS):
                            scatter(d_acc, den_ps[:, HEADS * j:HEADS * (j + 1)], where, j, ALU.add)
                        order.leave(was, rounds)
                    rounds_loop(nc.vector, rounds, one)

                with nc.vector.Fori(0, NG, 1) as g:
                    it = order.enter(g, 2 * rounds * (extra + 4 + PAIRS))
                    for h in range(2):
                        sum_half(g, h)
                    order.leave(it, NG)
                merge(d_acc, ALU.add)
                per = P // BLK
                for q in range(per):
                    have = len(range(q, NBLK, per))
                    mark(cp(den[BLK * q:BLK * (q + 1), 0:have, :], t32[:, q::per, :]))
                order.wait()
                link(ts(den[:], den[:], DEN_EPS, None, ALU.add))
                link(nc.vector.reciprocal(den[:], den[:]))
                overlaps(STEPS)
                for t in range(NT):
                    r = ROWS[t]
                    dve.wait_ge(s_xt, NT + t + 1)
                    link(tt(nrm[0:r, t, :].rearrange("p (f o) -> p f o", o=OUT_F),
                            ps[0:r, t % 4, 0:P].rearrange("p (f o) -> p f o", o=OUT_F),
                            den[0:r, t, :].unsqueeze(2).to_broadcast([r, HEADS, OUT_F]), ALU.mult))
                    tt(nrm[0:r, t, :], nrm[0:r, t, :], xs[0:r, t, :], ALU.add).then_inc(s_fin, 1)

            mark(nc.vector.memset(xs[:, NT - 1, :], 0.0))
            order.wait()
            nc.vector.memset(eps[:], LN_EPS).then_inc(s_const, 1)
            nc.vector.memset(neg_big[:], -BIG)
            for table in (col_tab, look_tab, acc_tab):
                last = nc.vector.memset(table[:], 0)
            link(last)
            nc.vector.memset(zeros[:], 0.0)
            nc.vector.memset(look_a[:], 0.0)
            nc.vector.memset(look_b[:], 0.0)
            nc.vector.memset(d_acc[:], 0.0)
            nc.vector.memset(den[:], 1.0)
            nc.vector.memset(m_acc[:], -BIG)
            nc.vector.memset(over[:], 0.0).then_inc(s_used[0], 1)
            nc.vector.memset(scr[:, 0, 0:1], 0.0).then_inc(s_used[1], 1)
            dve.wait_ge(s_pool, 5)
            for k in range(4):
                cp(ident4[:, k, :], ident[:])
            cp(start_f[:], start_i[:])
            mark(cp(iota[:], iota_i[:]))
            order.wait()
            nc.vector.memset(scr[:, 0, 1:2], 0.0).then_inc(s_const, 1)
            dve.wait_ge(s_ld_e, 80)
            link(cp(rows_f[:], rows_i[:]))
            mark(nc.vector.tensor_reduce(dmax[:], rows_f[:], AX.X, ALU.max))
            link(nc.vector.tensor_reduce(dmin[:], rows_f[:], AX.X, ALU.min))
            link(cp(win_i[:], dmin[:]))
            link(ts(win_i[:], win_i[:], 5, None, ALU.arith_shift_right))
            mark(cp(win_f[:], win_i[:]))
            order.wait()
            link(stt(over[:, 0:4], win_f[:], -float(BLK), dmax[:], ALU.mult, ALU.add))
            nc.vector.tensor_reduce(over[:, 4:5], over[:, 0:4], AX.X, ALU.max).then_inc(s_win, 1)
            mark(cp(dst_f[:], dst_i[:]))
            mark(cp(src_f[:], src_i[:]))
            link(nc.vector.tensor_reduce(tmp_e[:], attr[:], AX.X, ALU.max))
            mark(tt(etype[:], attr[:, :, 2], tmp_e[:], ALU.is_lt))
            mark(tt(rel[:], attr[:, :, 1], tmp_e[:], ALU.is_lt))
            link(tt(tmp_e[:], attr[:, :, 0], tmp_e[:], ALU.is_lt))
            link(stt(etype[:], etype[:], 1.0, rel[:], ALU.add, ALU.mult))
            link(stt(etype[:], etype[:], 1.0, tmp_e[:], ALU.add, ALU.mult))
            link(stt(idx0[:], src_f[:], float(TYPES), etype[:], ALU.mult, ALU.add))
            dve.wait_ge(s_winb, 1)
            link(cp(blk_f[:], ps[:, 0, 0:TILES]))
            mark(stt(rel[:], blk_f[:], -float(BLK), dst_f[:], ALU.mult, ALU.add))
            halves = blk_f[0:1, :].rearrange("p (i k) -> p i k", k=HALF)
            mark(ts(look_tab[:, :, 0:HALF], halves, float(2 * HEADS), None, ALU.mult))
            mark(ts(acc_tab[:, :, 0:HALF], halves, float(HEADS), None, ALU.mult))
            link(ts(col_f[:], blk_f[0:1, :], float(OWN // BLK), None, ALU.is_ge))
            for b in range(2, CHUNKS):
                link(stt(col_f[:], blk_f[0:1, :], float(OWN // BLK * b), col_f[:], ALU.is_ge, ALU.add))
            link(ts(col_f[:], col_f[:], float(BANK - OWN), None, ALU.mult))
            link(stt(col_tab[:, :, 0:HALF], halves, float(BLK), col_f[:].rearrange("p (i k) -> p i k", k=HALF),
                     ALU.mult, ALU.add))
            dve.wait_ge(s_winb, 2)
            link(nc.vector.tensor_reduce(narrow_f[:, 0:1], ps[0:1, 1, 0:NQ], AX.X, ALU.max))
            link(ts(narrow[:], narrow_f[:, 0:1], float(WIN), None, ALU.is_lt))
            dve.wait_ge(s_ld_w, 16 * 8)
            mark(tt(bgh[:, 0:2], bih_s[:, 0:2], bhh_s[:, 0:2], ALU.add))
            mark(cp(bgh[:, 2:3], bhh_s[:, 2:3]))
            w1v = w1_s[:, 0:D].rearrange("p (f o) -> p f o", o=OUT_F)
            for k in range(2):
                mark(tt(wa[:, k, :, :], w1v, a_s[:, k, :, :], ALU.mult))
            order.wait()
            for k in range(2):
                mark(nc.vector.tensor_reduce(w1_s[:, D + HEADS * k:D + HEADS * (k + 1)], wa[:, k, :, :], AX.X, ALU.add))
            order.wait()
            dve.wait_ge(s_ld_x, 32)
            norm(0)
            dve.wait_ge(s_relu, NT)
            nc.vector.memset(dlt[:, 0:1], 0.0).then_inc(s_h, CHUNKS)
            nc.vector.memset(dlt[:, 1:2], 0.0).then_inc(s_flag, 1)
            either(dve, program, order)


_INS = ["x", "src_t", "dst_t", "dst_rows", "attr_t", "ew_t", "we_t", "be", "wih_t", "whh_t", "bih", "bhh", "w1", "a1"]


def kernel(x, src, dst, edge_attr_4, edge_weight, L0_gnn_W_edge, L0_gnn_b_edge, L0_gnn_W_ih, L0_gnn_W_hh,
           L0_gnn_b_ih, L0_gnn_b_hh, L1_gnn_W, L1_gnn_a):
    import numpy as np
    import concourse.bacc as bacc
    from concourse.bass_utils import run_bass_kernel_spmd

    arr = [np.asarray(v) for v in (x, src, dst, edge_attr_4, edge_weight, L0_gnn_W_edge, L0_gnn_b_edge, L0_gnn_W_ih,
                                   L0_gnn_W_hh, L0_gnn_b_ih, L0_gnn_b_hh, L1_gnn_W, L1_gnn_a)]
    x, src, dst, attr, ew, we, be, wih, whh, bih, bhh, w1, a1 = arr
    pad = TILES * P - E
    src = np.concatenate([src, np.zeros(pad, src.dtype)])
    dst = np.concatenate([dst, np.full(pad, NP - 1, dst.dtype)])
    ew = np.concatenate([ew, np.zeros(pad, ew.dtype)])
    attr = np.concatenate([attr, np.zeros((pad, TYPES), attr.dtype)])
    data = {
        "x": x,
        "src_t": src.reshape(TILES, P).T,
        "dst_t": dst.reshape(TILES, P).T,
        "dst_rows": dst.reshape(4, NQ, P).transpose(1, 0, 2),
        "attr_t": attr.reshape(TILES, P, TYPES).transpose(1, 0, 2),
        "ew_t": ew.reshape(TILES, P).T,
        "we_t": we.reshape(TYPES * D, D).T,
        "be": be.reshape(TYPES * D),
        "wih_t": wih.T,
        "whh_t": whh.T,
        "bih": bih.reshape(3, D).T,
        "bhh": bhh.reshape(3, D).T,
        "w1": w1.transpose(1, 0, 2).reshape(D, HEADS * OUT_F),
        "a1": a1.reshape(HEADS, 2, OUT_F).transpose(1, 0, 2),
    }
    nc = bacc.Bacc("TRN2", target_bir_lowering=False, num_devices=1)
    arrays, args = {}, []
    for name in _INS:
        a = np.ascontiguousarray(data[name])
        arrays[f"in_{name}"] = a
        args.append(nc.dram_tensor(f"in_{name}", a.shape, mybir.dt.from_np(a.dtype), kind="ExternalInput").ap())
    args.append(nc.dram_tensor("out_0", (N, D), fp32, kind="ExternalOutput").ap())
    gnn_kernel(nc, *args)
    r = run_bass_kernel_spmd(nc, [arrays], core_ids=[0])
    return r.results[0]["out_0"]
```

```python
from contextlib import ExitStack

import concourse.bass as bass
from concourse import mybir

fp32 = mybir.dt.float32
bf16 = mybir.dt.bfloat16
i32 = mybir.dt.int32
ALU = mybir.AluOpType
ACT = mybir.ActivationFunctionType
AX = mybir.AxisListType

P = 128
N, E, D = 3125, 50000, 128
TYPES, STEPS = 4, 4
HEADS, OUT_F = 4, 32
SLOPE, LN_EPS, DEN_EPS = 0.2, 1e-5, 1e-16
WIN, BLK = 64, 32
BANK = 512
OWN = BANK - WIN
CHUNKS = -(-N // OWN)
NP = CHUNKS * OWN
NT = -(-NP // P)
ROWS = [min(P, NP - P * t) for t in range(NT)]
NBLK = NP // BLK
NWIN = NP // WIN
NG, HALF = 14, 14
G = 2 * HALF
TILES = NG * G
QT = HALF // 2
PAIRS = HALF // 2
RING = 5
SCORES = HALF * HEADS
R1 = D + HEADS
BIG = 2.0 ** 100
REGS = 16
NQ = TILES // 4
assert NG * G >= -(-E // P) and NQ <= P and NP >= N


class Order:

    def __init__(self, eng, sem):
        self.eng, self.sem, self.n, self.loops = eng, sem, 0, 0

    def mark(self, ins):
        ins.then_inc(self.sem, 1)
        self.n += 1

    def wait(self):
        self.eng.wait_ge(self.sem, self.loops + self.n)

    def link(self, ins):
        self.mark(ins)
        self.wait()

    def enter(self, i, per):
        was = (self.loops, self.n, per)
        self.loops = self.loops + i * per
        return was

    def leave(self, was, count):
        loops, n, per = was
        assert self.n - n == per, (self.n - n, per)
        self.loops, self.n = loops, n + per * count


def gnn_kernel(nc, x, src_t, dst_t, dst_rows, attr_t, ew_t, we_t, be, wih_t, whh_t, bih, bhh, w1, a1, out,
               force_rounds=None):
    ctx = ExitStack()
    with ctx:
        def sb(name, shape, dt=fp32):
            return ctx.enter_context(nc.sbuf_tensor(name, shape, dt))

        def sem(name):
            return ctx.enter_context(nc.semaphore(name))

        tab0 = nc.dram_tensor("tab0", (NP * TYPES, D), fp32, kind="Internal").ap()
        tab1 = nc.dram_tensor("tab1", (NP, D), fp32, kind="Internal").ap()
        tab_s = nc.dram_tensor("tab_s", (NP, HEADS), fp32, kind="Internal").ap()
        tab_t = nc.dram_tensor("tab_t", (NP, HEADS), fp32, kind="Internal").ap()

        src_i = sb("src_i", [P, TILES + G], i32)
        dst_i = sb("dst_i", [P, TILES], i32)
        rows_i = sb("rows_i", [NQ, 4, P], i32)
        attr = sb("attr", [P, TILES, TYPES])
        ew = sb("ew", [P, TILES])
        src_f = sb("src_f", [P, TILES])
        dst_f = sb("dst_f", [P, TILES])
        rel = sb("rel", [P, TILES])
        idx0 = sb("idx0", [P, TILES], i32)
        etype = sb("etype", [P, TILES])
        tmp_e = sb("tmp_e", [P, TILES])
        rows_f = sb("rows_f", [NQ, 4, P])
        dmin = sb("dmin", [NQ, 4])
        dmax = sb("dmax", [NQ, 4])
        win_i = sb("win_i", [NQ, 4], i32)
        win_f = sb("win_f", [NQ, 4])
        over = sb("over", [NQ, 5])
        blk_f = sb("blk_f", [P, TILES])
        col_f = sb("col_f", [1, TILES])
        col_tab = sb("col_tab", [1, 2 * NG, REGS], i32)
        blk_tab = sb("blk_tab", [1, 2 * NG, REGS], i32)
        narrow_f = sb("narrow_f", [1, 2])
        narrow = sb("narrow", [1, 1], i32)
        ident = sb("ident", [P, P])
        ident4 = sb("ident4", [P, 4, P], bf16)
        iota_i = sb("iota_i", [P, WIN], i32)
        iota = sb("iota", [P, WIN])
        start_i = sb("start_i", [P, NWIN], i32)
        start_f = sb("start_f", [P, NWIN])
        start_col = sb("start_col", [1, NWIN], i32)
        zeros = sb("zeros", [P, BANK], bf16)
        eps = sb("eps", [P, 1])
        neg_big = sb("neg_big", [P, 1])
        one = sb("one", [P, 1])
        xs = sb("xs", [P, NT, D])
        nrm = sb("nrm", [P, NT, D])
        stats = sb("stats", [P, NT, 6])
        mv = sb("mv", [P, NT, 2])
        rstd = sb("rstd", [P, NT])
        h_t = sb("h_t", [P, NP])
        agg_t = sb("agg_t", [P, NP])
        spill = sb("spill", [P, CHUNKS, WIN])
        gh = sb("gh", [P, 3, NP])
        over_gh = gh[:, :, :].rearrange("p g n -> p (g n)")
        n_pick, n_wmsg, n_hot_t = PAIRS * HEADS * P // 2, G * D, PAIRS * P
        pick = over_gh[0:2 * SCORES, 0:n_pick].bitcast(bf16).rearrange("p (j f b n) -> p j f b n", j=PAIRS, f=HEADS, b=2)
        wmsg = over_gh[:, n_pick:n_pick + n_wmsg].rearrange("p (k d) -> p k d", d=D)
        hot_t = over_gh[:, n_pick + n_wmsg:n_pick + n_wmsg + n_hot_t].rearrange("p (j e) -> p j e", e=P)
        rz = sb("rz", [P, 3, 2, OWN])
        cand = sb("cand", [P, 2, OWN])
        dlt = sb("dlt", [P, OWN])
        we_s = sb("we_s", [P, TYPES * D])
        be_s = sb("be_s", [P, TYPES * D])
        wih_s = sb("wih_s", [P, 3 * D])
        whh_s = sb("whh_s", [P, 3 * D])
        bih_s = sb("bih_s", [P, 3])
        bhh_s = sb("bhh_s", [P, 3])
        bgh = sb("bgh", [P, 3])
        w1_s = sb("w1_s", [P, D + 2 * HEADS])
        a_s = sb("a_s", [P, 2, HEADS, OUT_F])
        wa = sb("wa", [P, 2, HEADS, OUT_F])
        stage = [sb(f"stage{h}", [P, HALF], i32) for h in range(2)]
        msg = sb("msg", [P, G, D])
        srow = sb("srow", [P, G, HEADS])
        hot = sb("hot", [P, G, WIN])
        neg = sb("neg", [P, G, WIN], bf16)
        rel_w = sb("rel_w", [P, G])
        tabst = sb("tabst", [P, 3, TYPES * D])
        scr = sb("scr", [P, HALF, HEADS])
        lgt = sb("lgt", [P, HALF, HEADS])
        logits = sb("logits", [P, TILES, HEADS])
        etg = sb("etg", [P, HALF, HEADS])
        parts = sb("parts", [P, 3, SCORES], bf16)
        part12_t = sb("part12_t", [2 * SCORES, P], bf16)
        part3_t = sb("part3_t", [SCORES, P], bf16)
        ex = sb("ex", [P, G, HEADS])
        pmax = sb("pmax", [P, PAIRS, HEADS])
        m_acc = sb("m_acc", [P, NBLK * HEADS])
        d_acc = sb("d_acc", [P, NBLK * HEADS])
        look_a = sb("look_a", [P, NBLK, HEADS])
        look_b = sb("look_b", [P, NBLK, HEADS])
        t32 = sb("t32", [BLK, NBLK, HEADS])
        sh = sb("sh", [BLK, 3, NBLK, HEADS])
        den = sb("den", [P, NT, HEADS])

        ps = ctx.enter_context(nc.psum_tensor("ps", [P, 8, BANK], fp32))
        acc = ps[:, :, :].rearrange("p b c -> p (b c)")
        hot_ps = ps[:, 7, 0:n_hot_t // 2].bitcast(bf16).rearrange("p (j e) -> p j e", e=P)
        etg_ps = ps[:, RING, 0:SCORES]
        part_ps = ps[:, RING + 1, 0:P].bitcast(bf16).rearrange("p (b e) -> p b e", e=P)
        max_ps = ps[:, 7, 0:SCORES]
        den_ps = ps[:, 7, SCORES:SCORES + PAIRS * HEADS]

        s_ld_e, s_ld_x, s_ld_w = sem("s_ld_e"), sem("s_ld_x"), sem("s_ld_w")
        s_pool = sem("s_pool")
        s_const = sem("s_const")
        s_dve = sem("s_dve")
        s_win, s_winb, s_flag = sem("s_win"), sem("s_winb"), sem("s_flag")
        s_xt, s_var, s_sd, s_nrm, s_nt, s_relu = (sem(f"s_{n}") for n in ("xt", "var", "sd", "nrm", "nt", "relu"))
        s_xadd = sem("s_xadd")
        s_h = sem("s_h")
        s_tp, s_tf = sem("s_tp"), sem("s_tf")
        s_tw = [sem(f"s_tw{i}") for i in range(3)]
        s_gh, s_ghf = sem("s_gh"), sem("s_ghf")
        s_arr = [sem(f"s_arr{q}") for q in range(4)]
        s_idx = [sem(f"s_idx{h}") for h in range(2)]
        s_hot = [sem(f"s_hot{h}") for h in range(2)]
        s_used = [sem(f"s_used{h}") for h in range(2)]
        s_sum, s_ev, s_agg = sem("s_sum"), sem("s_ev"), sem("s_agg")
        s_gi, s_pre, s_sig, s_npre, s_tanh = (sem(f"s_{n}") for n in ("gi", "pre", "sig", "npre", "tanh"))
        s_lp, s_lf = sem("s_lp"), sem("s_lf")
        s_lw = [sem(f"s_lw{i}") for i in range(3)]
        s_t32, s_look, s_mx = sem("s_t32"), sem("s_look"), sem("s_mx")
        s_neg, s_otp, s_ot, s_lk = sem("s_neg"), sem("s_otp"), sem("s_ot"), sem("s_lk")
        s_lgt, s_ltp, s_lt, s_bc, s_bcf = sem("s_lgt"), sem("s_ltp"), sem("s_lt"), sem("s_bc"), sem("s_bcf")
        s_shift, s_ex, s_wm, s_den, s_denf = sem("s_shift"), sem("s_ex"), sem("s_wm"), sem("s_den"), sem("s_denf")
        s_fin, s_out, s_w = sem("s_fin"), sem("s_out"), sem("s_w")

        block = ctx.enter_context(nc.Block())

        def chunk_of(t):
            return (P * t + ROWS[t] - 1) // OWN

        def rounds_loop(eng, rounds, body):
            if rounds == 1:
                body(0)
            else:
                with eng.Fori(0, rounds, 1) as w:
                    body(w)

        def places(eng, table, g, h, top):
            loaded = nc.values_load_multi_w_load_instructions(
                table[0:1, bass.ds(g * 2 + h, 1), :].rearrange("p a b -> p (a b)"), engines=[eng.engine],
                min_val=0, max_val=top)[1]
            return loaded[0:HALF]

        def either(eng, program, order=None):
            eng.wait_ge(s_flag, 1)
            before = order.n if order else 0
            if force_rounds:
                return program(force_rounds)
            flag = eng.value_load(narrow[0:1, 0:1], min_val=0, max_val=1)
            with eng.If(flag):
                program(1)
            with eng.Else():
                if order:
                    order.n = before
                program(NWIN)

        def skewed(eng, rounds, start, work, finish, per_half=None):
            if rounds > 1:
                with eng.Fori(0, NG, 1) as g:
                    for h in range(2):
                        with eng.Fori(0, rounds, 1) as w:
                            start(g, h, w)
                            finish(g, h, w)
                            work(g, h, w)
                        if per_half:
                            per_half(g, h)
                return
            start(0, 0, 0)
            finish(0, 0, 0)
            with eng.Fori(0, NG - 1, 1) as g:
                start(g, 1, 0)
                work(g, 0, 0)
                finish(g, 1, 0)
                start(g + 1, 0, 0)
                work(g, 1, 0)
                finish(g + 1, 0, 0)
            start(NG - 1, 1, 0)
            work(NG - 1, 0, 0)
            finish(NG - 1, 1, 0)
            work(NG - 1, 1, 0)

        tab_uses = [len(range(i, NT, 3)) for i in range(3)]

        @block.sync
        def _(sp):
            sp.dma_start(rows_i[:], dst_rows).then_inc(s_ld_e, 16)
            sp.dma_start(src_i[:, 0:TILES], src_t).then_inc(s_ld_e, 16)
            sp.dma_start(src_i[:, TILES:TILES + G], src_t[:, 0:G]).then_inc(s_ld_e, 16)
            sp.dma_start(dst_i[:], dst_t).then_inc(s_ld_e, 16)
            sp.dma_start(attr[:], attr_t).then_inc(s_ld_e, 16)
            sp.dma_start(ew[:], ew_t).then_inc(s_ld_e, 16)
            sp.wait_ge(s_const, 1)
            full = N // P
            sp.dma_start(xs[:, 0:full, :], x[0:full * P, :].rearrange("(t p) d -> p t d", p=P)).then_inc(s_ld_x, 16)
            sp.dma_start(xs[0:N - full * P, full, :], x[full * P:N, :]).then_inc(s_ld_x, 16)
            for dst, src in ((we_s[:], we_t), (be_s[:], be.partition_broadcast(P)), (wih_s[:], wih_t),
                             (whh_s[:], whh_t), (bih_s[:], bih), (bhh_s[:], bhh),
                             (w1_s[:, 0:D], w1), (a_s[:], a1.partition_broadcast(P))):
                sp.dma_start(dst, src).then_inc(s_ld_w, 16)
            with nc.sync.Fori(0, STEPS, 1) as st:
                for t in range(NT):
                    sp.wait_ge(s_tf, st * NT + t + 1)
                    sp.dma_start(tab0[TYPES * P * t:TYPES * (P * t + ROWS[t]), :].rearrange("(p k) d -> p (k d)", k=TYPES),
                                 tabst[0:ROWS[t], t % 3, :]).then_inc(s_tw[t % 3], 16)
            for t in range(NT):
                sp.wait_ge(s_lf, t + 1)
                r, s = ROWS[t], slice(P * t, P * t + ROWS[t])
                sp.dma_start(tab1[s, :], tabst[0:r, t % 3, 0:D]).then_inc(s_lw[t % 3], 16)
                sp.dma_start(tab_s[s, :], tabst[0:r, t % 3, D:R1]).then_inc(s_lw[t % 3], 16)
                sp.dma_start(tab_t[s, :], tabst[0:r, t % 3, R1:R1 + HEADS]).then_inc(s_lw[t % 3], 16)
            for i in range(3):
                sp.wait_ge(s_lw[i], 48 * tab_uses[i])
            sp.dma_start(t32[:], tab_t.rearrange("(c p) h -> p c h", p=BLK)).then_inc(s_t32, 16)
            sp.wait_ge(s_fin, NT - 1)
            sp.dma_start(out[0:full * P, :].rearrange("(t p) d -> p t d", p=P), nrm[:, 0:full, :]).then_inc(s_out, 16)
            sp.wait_ge(s_fin, NT)
            sp.dma_start(out[full * P:N, :], nrm[0:N - full * P, full, :]).then_inc(s_out, 16)
            sp.wait_ge(s_out, 32)

        @block.gpsimd
        def _(pool):
            pool.iota(iota_i[:], pattern=[[1, WIN]], base=0, channel_multiplier=0).then_inc(s_pool, 1)
            pool.iota(start_i[:], pattern=[[WIN, NWIN]], base=0, channel_multiplier=0).then_inc(s_pool, 1)
            pool.iota(start_col[:], pattern=[[BANK, CHUNKS], [WIN, OWN // WIN]], base=0,
                      channel_multiplier=0).then_inc(s_pool, 1)
            pool.memset(ident[:], 0.0).then_inc(s_pool, 1)
            pool.wait_ge(s_pool, 4)
            pool.affine_select(out=ident[:], in_=ident[:], compare_op=ALU.not_equal, fill=1.0, base=0,
                               pattern=[[-1, P]], channel_multiplier=1).then_inc(s_pool, 1)

            def wait_on(sem, value):
                value = pool.snap(value)
                pool.keepalive_nop([pool.lower_val_access(value)])
                pool.wait_ge(s_pool, 5)
                pool.wait_ge(sem, value)

            def gathers(n, table, to):
                for h in range(2):
                    wait_on(s_idx[h], n + 1)
                    for k in range(HALF):
                        slot = h * HALF + k
                        pool.indirect_dma_start(to[:, slot, :], None, table,
                                                bass.IndirectOffsetOnAxis(stage[h][:, k:k + 1], 0)
                                                ).then_inc(s_arr[slot // QT], 16)

            with nc.gpsimd.Fori(0, STEPS, 1) as st:
                for i in range(3):
                    wait_on(s_tw[i], (st + 1) * (16 * tab_uses[i]))
                with nc.gpsimd.Fori(0, NG, 1) as g:
                    gathers(st * NG + g, tab0, msg)
            for i in range(3):
                pool.wait_ge(s_lw[i], 48 * tab_uses[i])
            with nc.gpsimd.Fori(0, NG, 1) as g:
                gathers(g + STEPS * NG, tab_s, srow)
            with nc.gpsimd.Fori(0, NG, 1) as g:
                gathers(g + (STEPS + 1) * NG, tab1, msg)

        @block.scalar
        def _(act):
            def norm(n):
                act.wait_ge(s_var, n + 1)
                act.activation(rstd[:], mv[:, :, 1], ACT.Sqrt, bias=eps[:, 0:1]).then_inc(s_sd, 1)
                for t in range(NT):
                    act.wait_ge(s_nt, n * NT + t + 1)
                    act.activation(h_t[:, P * t:P * t + ROWS[t]], ps[:, 4 + t % 4, 0:ROWS[t]],
                                   ACT.Relu).then_inc(s_relu, 1)

            def sum_out(st):
                for c in range(CHUNKS):
                    act.wait_ge(s_sum, st * CHUNKS + c + 1)
                    act.activation(agg_t[:, OWN * c:OWN * (c + 1)], ps[:, c, 0:OWN], ACT.Copy)
                    act.activation(spill[:, c, :], ps[:, c, OWN:BANK], ACT.Copy).then_inc(s_ev, 1)

            def program(rounds):
                with nc.scalar.Fori(0, STEPS, 1) as st:
                    for m in range(3 * CHUNKS):
                        g, c = m % 3, m // 3
                        act.wait_ge(s_gh, st * (3 * CHUNKS) + m + 1)
                        act.activation(gh[:, g, OWN * c:OWN * (c + 1)], ps[:, m % 6, 0:OWN], ACT.Identity,
                                       bias=bgh[:, g:g + 1]).then_inc(s_ghf, 1)
                    sum_out(st)
                    for i in range(CHUNKS + 1):
                        if i < CHUNKS:
                            act.wait_ge(s_pre, st * CHUNKS + i + 1)
                            act.activation(rz[:, i % 3, :, :], rz[:, i % 3, :, :], ACT.Sigmoid).then_inc(s_sig, 1)
                        if i >= 1:
                            act.wait_ge(s_npre, st * CHUNKS + i)
                            act.activation(cand[:, (i - 1) % 2, :], cand[:, (i - 1) % 2, :], ACT.Tanh,
                                           bias=bih_s[:, 2:3]).then_inc(s_tanh, 1)
                norm(1)
                for t in range(NT):
                    act.wait_ge(s_lp, t + 1)
                    if t >= 3:
                        act.wait_ge(s_lw[t % 3], 48 * (t // 3))
                    act.activation(tabst[0:ROWS[t], t % 3, 0:R1 + HEADS], ps[0:ROWS[t], t % 2, 0:R1 + HEADS],
                                   ACT.Copy).then_inc(s_lf, 1)

                def start(n_hot, n, h):
                    act.wait_ge(s_hot[h], n_hot)
                    act.activation(neg[:, h * HALF:(h + 1) * HALF, :], hot[:, h * HALF:(h + 1) * HALF, :],
                                   ACT.Identity, scale=BIG, bias=neg_big[:, 0:1]).then_inc(s_neg, 1)
                    act.wait_ge(s_otp, n + 1)
                    act.activation(hot_t[:], hot_ps, ACT.Identity, scale=1 / BIG, bias=one[:, 0:1]).then_inc(s_ot, 1)

                def max_start(g, h, w):
                    start((g + STEPS * NG) * rounds + w + 1, (g * 2 + h) * rounds + w, h)

                def max_finish(g, h, w):
                    act.wait_ge(s_ltp, (g * 2 + h) * rounds + w + 1)
                    act.activation(part12_t[:], part_ps[0:2 * SCORES, 0, :], ACT.Copy)
                    act.activation(part3_t[:], part_ps[0:SCORES, 1, :], ACT.Copy).then_inc(s_lt, 1)

                def sum_start(g, h, w):
                    start((g + (STEPS + 1) * NG) * rounds + w + 1, 2 * NG * rounds + (g * 2 + h) * rounds + w, h)

                def sum_finish(g, h, w):
                    act.wait_ge(s_shift, (g * 2 + h) * rounds + w + 1)
                    act.activation(ex[:, h * HALF:(h + 1) * HALF, :], lgt[:], ACT.Exp).then_inc(s_ex, 1)

                skewed(nc.scalar, rounds, max_start, lambda g, h, w: None, max_finish)
                skewed(nc.scalar, rounds, sum_start, lambda g, h, w: None, sum_finish)
                sum_out(STEPS)

            act.wait_ge(s_const, 2)
            norm(0)
            either(act, program)

        @block.tensor
        def _(pe):
            mm = nc.tensor.matmul

            def norm(n):
                if n:
                    pe.wait_ge(s_npre, CHUNKS * STEPS)
                    for t in range(NT):
                        pe.wait_ge(s_h, CHUNKS * STEPS + chunk_of(t) + 1)
                        if t >= 4:
                            pe.wait_ge(s_xadd, t - 3)
                        nc.tensor.transpose(ps[0:ROWS[t], t % 4, 0:P], h_t[:, P * t:P * t + ROWS[t]],
                                            ident[:]).then_inc(s_xt, 1)
                for t in range(NT):
                    pe.wait_ge(s_nrm, n * NT + t + 1)
                    if t >= 4:
                        pe.wait_ge(s_relu, n * NT + t - 3)
                    nc.tensor.transpose(ps[:, 4 + t % 4, 0:ROWS[t]], nrm[0:ROWS[t], t, :],
                                        ident[0:ROWS[t], 0:ROWS[t]]).then_inc(s_nt, 1)

            def open_sums():
                for c in range(CHUNKS):
                    mm(ps[:, c, :], zeros[:, 0:P], zeros[:], start=True, stop=False)

            def close_sums():
                for c in range(CHUNKS):
                    mm(ps[:, c, :], zeros[:, 0:P], zeros[:], start=False, stop=True).then_inc(s_sum, 1)

            def program(rounds):
                def columns(g, h, w):
                    top = CHUNKS * BANK - WIN
                    if rounds == 1:
                        return places(pe, col_tab, g, h, top)
                    return [pe.value_load(start_col[0:1, bass.ds(w, 1)], min_val=0, max_val=top)] * HALF

                def node_places(g, h, w):
                    if rounds == 1:
                        return places(pe, blk_tab, g, h, HEADS * (NBLK - 1))
                    return [w * (2 * HEADS)] * HALF

                def add_half(n, g, h):
                    def one(w):
                        for q in (2 * h, 2 * h + 1):
                            pe.wait_ge(s_arr[q], (n + 1) * (16 * QT))
                        pe.wait_ge(s_hot[h], n * rounds + w + 1)
                        cols = columns(g, h, w)
                        for k in range(HALF):
                            slot = h * HALF + k
                            last = mm(acc[:, bass.ds(cols[k], WIN)], msg[:, slot, 0:D], hot[:, slot, :], start=False, stop=False)
                        last.then_inc(s_used[h], 1)
                    rounds_loop(nc.tensor, rounds, one)

                with nc.tensor.Fori(0, STEPS, 1) as st:
                    for t in range(NT):
                        pe.wait_ge(s_h, st * CHUNKS + chunk_of(t) + 1)
                        if t >= 2:
                            pe.wait_ge(s_tf, st * NT + t - 1)
                        mm(ps[0:ROWS[t], 6 + t % 2, :], h_t[:, P * t:P * t + ROWS[t]], we_s[:],
                           start=True, stop=True).then_inc(s_tp, 1)
                    for m in range(3 * CHUNKS):
                        g, c = m % 3, m // 3
                        if m >= 6:
                            pe.wait_ge(s_ghf, st * (3 * CHUNKS) + m - 5)
                        mm(ps[:, m % 6, 0:OWN], whh_s[:, D * g:D * (g + 1)], h_t[:, OWN * c:OWN * (c + 1)],
                           start=True, stop=True).then_inc(s_gh, 1)
                    pe.wait_ge(s_ghf, (st + 1) * (3 * CHUNKS))
                    pe.wait_ge(s_tf, (st + 1) * NT)
                    open_sums()
                    with nc.tensor.Fori(0, NG, 1) as g:
                        for h in range(2):
                            add_half(st * NG + g, g, h)
                    close_sums()
                    pe.wait_ge(s_ev, (st + 1) * CHUNKS)
                    for c in range(CHUNKS):
                        if c >= 1:
                            pe.wait_ge(s_agg, st * (CHUNKS - 1) + c)
                        if c >= 2:
                            pe.wait_ge(s_npre, st * CHUNKS + c - 1)
                        for g in range(3):
                            last = mm(ps[:, 3 * (c % 2) + g, 0:OWN], wih_s[:, D * g:D * (g + 1)],
                                      agg_t[:, OWN * c:OWN * (c + 1)], start=True, stop=True)
                        last.then_inc(s_gi, 1)
                norm(1)
                for t in range(NT):
                    pe.wait_ge(s_relu, NT + t + 1)
                    if t >= 2:
                        pe.wait_ge(s_lf, t - 1)
                    mm(ps[0:ROWS[t], t % 2, 0:R1 + HEADS], h_t[:, P * t:P * t + ROWS[t]], w1_s[:],
                       start=True, stop=True).then_inc(s_lp, 1)
                pe.wait_ge(s_lf, NT)

                def start(n, g, h, w, at):
                    where = node_places(g, h, w)
                    pe.wait_ge(s_neg, n + 1)
                    for j in range(PAIRS):
                        s0 = h * HALF + 2 * j
                        last = nc.tensor.transpose(hot_ps[:, j, :], neg[:, s0:s0 + 2, :].rearrange("p a b -> p (a b)"),
                                                   ident4[:, 0, :])
                    last.then_inc(s_otp, 1)
                    pe.wait_ge(s_ot, n + 1)
                    for k in range(HALF):
                        flat = (look_a, look_b)[k % 2][:, :, :].rearrange("p c f -> p (c f)")
                        last = mm(at[:, k * HEADS:(k + 1) * HEADS], hot_t[:, k // 2, :],
                                  flat[:, bass.ds(where[k], HEADS)], start=True, stop=True)
                    last.then_inc(s_lk, 1)

                def max_start(g, h, w):
                    start((g * 2 + h) * rounds + w, g, h, w, etg_ps)

                def max_finish(g, h, w):
                    have = pe.snap((g * 2 + h) * rounds + w + 1)
                    pe.wait_ge(s_look, 1)
                    pe.wait_ge(s_lgt, have)
                    nc.tensor.transpose(part_ps[0:2 * SCORES, 0, :], parts[:, 0:2, :].rearrange("p a b -> p (a b)"), ident4[:, 0, :])
                    nc.tensor.transpose(part_ps[0:SCORES, 1, :], parts[:, 2, :], ident4[:, 0, :]).then_inc(s_ltp, 1)

                def max_work(g, h, w):
                    n = (g * 2 + h) * rounds + w
                    pe.wait_ge(s_lt, n + 1)
                    for j in range(PAIRS):
                        bank = ps[:, j % RING, :]
                        if j >= RING:
                            pe.wait_ge(s_bcf, n * PAIRS + j - RING + 1)
                        s0 = h * HALF + 2 * j
                        mm(bank, neg[:, s0:s0 + 2, :].rearrange("p a b -> p (a b)"),
                           ident4[:].rearrange("p a b -> p (a b)"), start=True, stop=False)
                        for hd in range(HEADS):
                            at = bank[:, P * hd:P * (hd + 1)]
                            rows = pick[:, j, hd, :, :].rearrange("p a b -> p (a b)")
                            mm(at, rows, part12_t[:], start=False, stop=False)
                            last = mm(at, rows[0:SCORES, :], part3_t[:], start=False, stop=(hd == HEADS - 1))
                        last.then_inc(s_bc, 1)

                pe.wait_ge(s_look, 1)
                skewed(nc.tensor, rounds, max_start, max_work, max_finish)
                pe.wait_ge(s_look, 2)
                open_sums()

                def sum_start(g, h, w):
                    start(2 * NG * rounds + (g * 2 + h) * rounds + w, g, h, w, max_ps)

                def sum_finish(g, h, w):
                    pe.wait_ge(s_ex, (g * 2 + h) * rounds + w + 1)
                    for k in range(HALF):
                        slot = h * HALF + k
                        lo = WIN * (k % 2)
                        last = mm(den_ps[lo:lo + WIN, HEADS * (k // 2):HEADS * (k // 2 + 1)], hot[:, slot, :], ex[:, slot, :],
                                  start=True, stop=True)
                    last.then_inc(s_den, 1)

                def sum_work(g, h, w):
                    cols = columns(g, h, w)
                    pe.wait_ge(s_wm, (g * 2 + h) * rounds + w + 1)
                    for k in range(HALF):
                        slot = h * HALF + k
                        last = mm(acc[:, bass.ds(cols[k], WIN)], wmsg[:, slot, :], hot[:, slot, :], start=False, stop=False)
                    last.then_inc(s_used[h], 1)

                skewed(nc.tensor, rounds, sum_start, sum_work, sum_finish)
                close_sums()
                pe.wait_ge(s_ev, (STEPS + 1) * CHUNKS)
                for t in range(NT):
                    c = chunk_of(t)
                    if c >= 1:
                        pe.wait_ge(s_agg, STEPS * (CHUNKS - 1) + c)
                    if t >= 4:
                        pe.wait_ge(s_fin, t - 3)
                    nc.tensor.transpose(ps[0:ROWS[t], t % 4, 0:P], agg_t[:, P * t:P * t + ROWS[t]],
                                        ident[:]).then_inc(s_xt, 1)

            pe.wait_ge(s_pool, 5)
            pe.wait_ge(s_const, 2)
            pe.wait_ge(s_win, 1)
            for q in range(4):
                last = mm(ps[:, 0, NQ * q:NQ * (q + 1)], win_f[:, q:q + 1].to_broadcast([NQ, P]),
                          ident[0:NQ, 0:NQ], start=True, stop=True)
            last.then_inc(s_winb, 1)
            nc.tensor.transpose(ps[0:1, 1, 0:NQ], over[:, 4:5], ident[0:NQ, 0:NQ]).then_inc(s_winb, 1)
            norm(0)
            either(pe, program)

        @block.vector
        def _(dve):
            order = Order(dve, s_dve)
            link, mark = order.link, order.mark
            tt, ts, stt, cp = nc.vector.tensor_tensor, nc.vector.tensor_scalar, nc.vector.scalar_tensor_tensor, nc.vector.tensor_copy

            def norm(n):
                for t in range(NT):
                    if n:
                        dve.wait_ge(s_xt, t + 1)
                        tt(xs[0:ROWS[t], t, :], xs[0:ROWS[t], t, :], ps[0:ROWS[t], t % 4, 0:P], ALU.add).then_inc(s_xadd, 1)
                        dve.wait_ge(s_xadd, t + 1)
                    nc.vector.bn_stats(stats[:, t, :], xs[:, t, :]).then_inc(s_dve, 1)
                    order.n += 1
                order.wait()
                for t in range(NT):
                    last = nc.vector.bn_aggr(mv[:, t, :], stats[:, t, :])
                last.then_inc(s_var, 1)
                dve.wait_ge(s_sd, n + 1)
                link(nc.vector.reciprocal(rstd[:], rstd[:]))
                for t in range(NT):
                    ts(nrm[:, t, :], xs[:, t, :], mv[:, t, 0:1], rstd[:, t:t + 1], ALU.subtract, ALU.mult).then_inc(s_nrm, 1)

            def overlaps(st):
                dve.wait_ge(s_ev, (st + 1) * CHUNKS)
                for c in range(1, CHUNKS):
                    tt(agg_t[:, OWN * c:OWN * c + WIN], agg_t[:, OWN * c:OWN * c + WIN], spill[:, c - 1, :],
                       ALU.add).then_inc(s_agg, 1)

            def program(rounds):
                def acc_places(g, h, w):
                    if rounds == 1:
                        return places(dve, blk_tab, g, h, HEADS * (NBLK - 1))
                    return [w * (2 * HEADS)] * HALF

                def free_half(n, h, w):
                    dve.wait_ge(s_used[h], n * rounds + w + 1)

                def build_hot(n, g, h, w):
                    sl = slice(h * HALF, (h + 1) * HALF)
                    if rounds == 1:
                        r = rel[:, bass.ds(g * G + h * HALF, HALF)]
                    else:
                        link(ts(rel_w[:, sl], dst_f[:, bass.ds(g * G + h * HALF, HALF)], start_f[:, bass.ds(w, 1)], None,
                                ALU.subtract))
                        r = rel_w[:, sl]
                    tt(hot[:, sl, :], iota[:].unsqueeze(1).to_broadcast([P, HALF, WIN]),
                       r.unsqueeze(2).to_broadcast([P, HALF, WIN]), ALU.is_equal).then_inc(s_hot[h], 1)

                def stage_idx(n, g, h, idx):
                    cp(stage[h][:], idx[:, bass.ds(g * G + h * HALF, HALF)]).then_inc(s_idx[h], 1)

                extra = 0 if rounds == 1 else 1

                with nc.vector.Fori(0, STEPS, 1) as st:
                    step = order.enter(st, extra * 2 * NG * rounds + 3 * CHUNKS)
                    for t in range(NT):
                        dve.wait_ge(s_tp, st * NT + t + 1)
                        if t >= 3:
                            dve.wait_ge(s_tw[t % 3], st * (16 * tab_uses[t % 3]) + 16 * (t // 3))
                        tt(tabst[0:ROWS[t], t % 3, :], ps[0:ROWS[t], 6 + t % 2, :], be_s[0:ROWS[t], :], ALU.add).then_inc(s_tf, 1)
                    with nc.vector.Fori(0, NG, 1) as g:
                        it = order.enter(g, extra * 2 * rounds)
                        for h in range(2):
                            n = st * NG + g
                            free_half(n, h, 0)
                            stage_idx(n, g, h, idx0)

                            def one(w):
                                was = order.enter(w, extra)
                                free_half(n, h, w)
                                build_hot(n, g, h, w)
                                order.leave(was, rounds)
                            rounds_loop(nc.vector, rounds, one)
                        order.leave(it, NG)
                    overlaps(st)
                    for i in range(CHUNKS + 2):
                        if i < CHUNKS:
                            c = i
                            dve.wait_ge(s_gi, st * CHUNKS + c + 1)
                            if c >= 3:
                                dve.wait_ge(s_h, (st + 1) * CHUNKS + c - 2)
                            for g in range(2):
                                last = tt(rz[:, c % 3, g, :], ps[:, 3 * (c % 2) + g, 0:OWN], gh[:, g, OWN * c:OWN * (c + 1)], ALU.add)
                            last.then_inc(s_pre, 1)
                        if 1 <= i <= CHUNKS:
                            c = i - 1
                            dve.wait_ge(s_sig, st * CHUNKS + c + 1)
                            if c >= 2:
                                dve.wait_ge(s_h, (st + 1) * CHUNKS + c - 1)
                            link(tt(cand[:, c % 2, :], rz[:, c % 3, 0, :], gh[:, 2, OWN * c:OWN * (c + 1)], ALU.mult))
                            tt(cand[:, c % 2, :], cand[:, c % 2, :], ps[:, 3 * (c % 2) + 2, 0:OWN], ALU.add).then_inc(s_npre, 1)
                        if i >= 2:
                            c = i - 2
                            own = slice(OWN * c, OWN * (c + 1))
                            dve.wait_ge(s_tanh, st * CHUNKS + c + 1)
                            if c >= 1:
                                dve.wait_ge(s_h, (st + 1) * CHUNKS + c)
                            link(tt(dlt[:], h_t[:, own], cand[:, c % 2, :], ALU.subtract))
                            link(tt(dlt[:], dlt[:], rz[:, c % 3, 1, :], ALU.mult))
                            tt(h_t[:, own], cand[:, c % 2, :], dlt[:], ALU.add).then_inc(s_h, 1)
                    order.leave(step, STEPS)
                for h in range(2):
                    free_half(STEPS * NG, h, 0)
                    stage_idx(STEPS * NG, 0, h, src_i)
                norm(1)

                def place():
                    for table, p0 in ((look_a, 0), (look_b, 2 * BLK)):
                        cp(table[p0:p0 + BLK, :, :], t32[:])
                        last = cp(table[p0 + BLK:p0 + 2 * BLK, 0:NBLK - 1, :], t32[:, 1:NBLK, :])
                    return last

                def merge(table, op):
                    v = table[:].rearrange("p (c f) -> p c f", f=HEADS)
                    for q in range(3):
                        mark(cp(sh[:, q, :, :], v[BLK * (q + 1):BLK * (q + 2), :, :]))
                    order.wait()
                    link(tt(t32[:], v[0:BLK, :, :], sh[:, 1, :, :], op))
                    link(tt(t32[:, 1:, :], t32[:, 1:, :], sh[:, 0, 0:NBLK - 1, :], op))
                    link(tt(t32[:, 1:, :], t32[:, 1:, :], sh[:, 2, 0:NBLK - 1, :], op))

                first, second = (ident[0:2 * SCORES, SCORES * i:SCORES * (i + 1)].rearrange("p (j b f) -> p j b f", b=2, f=HEADS)
                                 for i in range(2))
                for b in range(2):
                    for j in range(PAIRS):
                        last = tt(pick[:, j, :, b, :], first[:, j, b, :].unsqueeze(2).to_broadcast([2 * SCORES, HEADS, WIN]),
                                  second[:, j, b, :].unsqueeze(2).to_broadcast([2 * SCORES, HEADS, WIN]), ALU.add)
                mark(last)
                dve.wait_ge(s_t32, 16)
                place().then_inc(s_look, 1)

                def logits_of(to, g, h, target):
                    link(tt(scr[:], target, srow[:, h * HALF:(h + 1) * HALF, :], ALU.add))
                    link(stt(lgt[:], scr[:], SLOPE, scr[:], ALU.mult, ALU.max))
                    return tt(to, lgt[:], ew[:, bass.ds(g * G + h * HALF, HALF)].unsqueeze(2).to_broadcast([P, HALF, HEADS]), ALU.mult)

                def stored(g, h):
                    return logits[:, bass.ds(g * G + h * HALF, HALF), :]

                def scatter(table, part, where, j, op):
                    order.wait()
                    for b in range(2):
                        lo = WIN * b
                        at = table[lo:lo + WIN, bass.ds(where[2 * j + b], HEADS)]
                        last = tt(at, at, part[lo:lo + WIN, :], op)
                    mark(last)

                def max_start(g, h, w):
                    build_hot(g + STEPS * NG, g, h, w)

                def next_rows(g, h, n):
                    stage_idx(n + 1, g + 1, h, src_i)

                def max_finish(g, h, w):
                    n = (g * 2 + h) * rounds + w
                    for q in (2 * h, 2 * h + 1):
                        dve.wait_ge(s_arr[q], (g + STEPS * NG + 1) * (16 * QT))
                    dve.wait_ge(s_lk, n + 1)
                    target = etg_ps.rearrange("p (k f) -> p k f", f=HEADS)
                    if rounds > 1:
                        mark(tt(etg[:], etg[:], target, ALU.add))
                    link(logits_of(lgt[:], g, h, target))
                    flat = lgt[:].rearrange("p k f -> p (k f)")
                    rest = scr[:].rearrange("p k f -> p (k f)")
                    if rounds == 1:
                        cp(stored(g, h), lgt[:])
                    link(cp(parts[:, 0, :], flat))
                    link(tt(rest, flat, parts[:, 0, :], ALU.subtract))
                    link(cp(parts[:, 1, :], rest))
                    tt(parts[:, 2, :], rest, parts[:, 1, :], ALU.subtract).then_inc(s_lgt, 1)
                    if rounds == 1:
                        next_rows(g, h, g + STEPS * NG)

                def max_half(g, h):
                    order.wait()
                    link(logits_of(lgt[:], g, h, etg[:]))
                    mark(cp(stored(g, h), lgt[:]))
                    link(nc.vector.memset(etg[:], 0.0))
                    next_rows(g, h, g + STEPS * NG)

                def max_work(g, h, w):
                    n = (g * 2 + h) * rounds + w
                    where = acc_places(g, h, w)
                    for j in range(PAIRS + 1):
                        if j < PAIRS:
                            dve.wait_ge(s_bc, n * PAIRS + j + 1)
                            nc.vector.tensor_reduce(pmax[:, j, :], ps[:, j % RING, :].rearrange("p (f e) -> p f e", e=P),
                                                    AX.X, ALU.max).then_inc(s_bcf, 1)
                        if j >= 1:
                            dve.wait_ge(s_bcf, n * PAIRS + j)
                            scatter(m_acc, pmax[:, j - 1, :], where, j - 1, ALU.max)

                def sweep(start, work, finish, per, per_half=None, per_end=0):
                    if rounds > 1:
                        with nc.vector.Fori(0, NG, 1) as g:
                            it = order.enter(g, 2 * (rounds * per + per_end))
                            for h in range(2):
                                with nc.vector.Fori(0, rounds, 1) as w:
                                    was = order.enter(w, per)
                                    start(g, h, w)
                                    finish(g, h, w)
                                    work(g, h, w)
                                    order.leave(was, rounds)
                                if per_half:
                                    per_half(g, h)
                            order.leave(it, NG)
                        return
                    start(0, 0, 0)
                    finish(0, 0, 0)
                    with nc.vector.Fori(0, NG - 1, 1) as g:
                        it = order.enter(g, 2 * per)
                        start(g, 1, 0)
                        work(g, 0, 0)
                        finish(g, 1, 0)
                        start(g + 1, 0, 0)
                        work(g, 1, 0)
                        finish(g + 1, 0, 0)
                        order.leave(it, NG - 1)
                    start(NG - 1, 1, 0)
                    work(NG - 1, 0, 0)
                    finish(NG - 1, 1, 0)
                    work(NG - 1, 1, 0)

                links = extra + (1 if rounds > 1 else 0)
                sweep(max_start, max_work, max_finish, links + 6 + PAIRS, max_half, 5)
                order.wait()
                merge(m_acc, ALU.max)
                place().then_inc(s_look, 1)

                def sum_start(g, h, w):
                    free_half(g + STEPS * NG, h, w)
                    build_hot(g + (STEPS + 1) * NG, g, h, w)

                def sum_finish(g, h, w):
                    n = (g * 2 + h) * rounds + w
                    where = acc_places(g, h, w)
                    dve.wait_ge(s_lk, 2 * NG * rounds + n + 1)
                    link(tt(lgt[:], stored(g, h), max_ps.rearrange("p (k f) -> p k f", f=HEADS), ALU.subtract))
                    ts(lgt[:], lgt[:], 0.0, None, ALU.min).then_inc(s_shift, 1)
                    dve.wait_ge(s_den, n + 1)
                    for j in range(PAIRS):
                        scatter(d_acc, den_ps[:, HEADS * j:HEADS * (j + 1)], where, j, ALU.add)

                def sum_work(g, h, w):
                    n = (g * 2 + h) * rounds + w
                    sl = slice(h * HALF, (h + 1) * HALF)
                    for q in (2 * h, 2 * h + 1):
                        dve.wait_ge(s_arr[q], (g + (STEPS + 1) * NG + 1) * (16 * QT))
                    dve.wait_ge(s_ex, n + 1)
                    tt(wmsg[:, sl, :].rearrange("p k (f o) -> p k f o", o=OUT_F), msg[:, sl, :].rearrange("p k (f o) -> p k f o", o=OUT_F),
                       ex[:, sl, :].unsqueeze(3).to_broadcast([P, HALF, HEADS, OUT_F]), ALU.mult).then_inc(s_wm, 1)
                    if rounds == 1:
                        next_rows(g, h, g + (STEPS + 1) * NG)

                def sum_half(g, h):
                    next_rows(g, h, g + (STEPS + 1) * NG)

                sweep(sum_start, sum_work, sum_finish, extra + 1 + PAIRS, sum_half)
                order.wait()
                merge(d_acc, ALU.add)
                per = P // BLK
                for q in range(per):
                    have = len(range(q, NBLK, per))
                    mark(cp(den[BLK * q:BLK * (q + 1), 0:have, :], t32[:, q::per, :]))
                order.wait()
                link(ts(den[:], den[:], DEN_EPS, None, ALU.add))
                link(nc.vector.reciprocal(den[:], den[:]))
                overlaps(STEPS)
                for t in range(NT):
                    r = ROWS[t]
                    dve.wait_ge(s_xt, NT + t + 1)
                    link(tt(nrm[0:r, t, :].rearrange("p (f o) -> p f o", o=OUT_F),
                            ps[0:r, t % 4, 0:P].rearrange("p (f o) -> p f o", o=OUT_F),
                            den[0:r, t, :].unsqueeze(2).to_broadcast([r, HEADS, OUT_F]), ALU.mult))
                    tt(nrm[0:r, t, :], nrm[0:r, t, :], xs[0:r, t, :], ALU.add).then_inc(s_fin, 1)

            mark(nc.vector.memset(xs[:, NT - 1, :], 0.0))
            order.wait()
            nc.vector.memset(eps[:], LN_EPS).then_inc(s_const, 1)
            nc.vector.memset(neg_big[:], -BIG)
            nc.vector.memset(one[:], 1.0)
            nc.vector.memset(etg[:], 0.0)
            nc.vector.memset(col_tab[:], 0)
            link(nc.vector.memset(blk_tab[:], 0))
            nc.vector.memset(zeros[:], 0.0)
            nc.vector.memset(look_a[:], 0.0)
            nc.vector.memset(look_b[:], 0.0)
            nc.vector.memset(d_acc[:], 0.0)
            nc.vector.memset(den[:], 1.0)
            nc.vector.memset(m_acc[:], -BIG)
            nc.vector.memset(over[:], 0.0).then_inc(s_used[0], 1)
            nc.vector.memset(scr[:, 0, 0:1], 0.0).then_inc(s_used[1], 1)
            dve.wait_ge(s_pool, 5)
            for k in range(4):
                cp(ident4[:, k, :], ident[:])
            cp(start_f[:], start_i[:])
            mark(cp(iota[:], iota_i[:]))
            order.wait()
            nc.vector.memset(scr[:, 0, 1:2], 0.0).then_inc(s_const, 1)
            dve.wait_ge(s_ld_e, 96)
            link(cp(rows_f[:], rows_i[:]))
            mark(nc.vector.tensor_reduce(dmax[:], rows_f[:], AX.X, ALU.max))
            link(nc.vector.tensor_reduce(dmin[:], rows_f[:], AX.X, ALU.min))
            link(cp(win_i[:], dmin[:]))
            link(ts(win_i[:], win_i[:], 5, None, ALU.arith_shift_right))
            mark(cp(win_f[:], win_i[:]))
            order.wait()
            link(stt(over[:, 0:4], win_f[:], -float(BLK), dmax[:], ALU.mult, ALU.add))
            nc.vector.tensor_reduce(over[:, 4:5], over[:, 0:4], AX.X, ALU.max).then_inc(s_win, 1)
            mark(cp(dst_f[:], dst_i[:]))
            mark(cp(src_f[:], src_i[:, 0:TILES]))
            link(nc.vector.tensor_reduce(tmp_e[:], attr[:], AX.X, ALU.max))
            mark(tt(etype[:], attr[:, :, 2], tmp_e[:], ALU.is_lt))
            mark(tt(rel[:], attr[:, :, 1], tmp_e[:], ALU.is_lt))
            link(tt(tmp_e[:], attr[:, :, 0], tmp_e[:], ALU.is_lt))
            link(stt(etype[:], etype[:], 1.0, rel[:], ALU.add, ALU.mult))
            link(stt(etype[:], etype[:], 1.0, tmp_e[:], ALU.add, ALU.mult))
            link(stt(idx0[:], src_f[:], float(TYPES), etype[:], ALU.mult, ALU.add))
            dve.wait_ge(s_winb, 1)
            link(cp(blk_f[:], ps[:, 0, 0:TILES]))
            mark(stt(rel[:], blk_f[:], -float(BLK), dst_f[:], ALU.mult, ALU.add))
            halves = blk_f[0:1, :].rearrange("p (i k) -> p i k", k=HALF)
            mark(ts(blk_tab[:, :, 0:HALF], halves, float(HEADS), None, ALU.mult))
            link(ts(col_f[:], blk_f[0:1, :], float(OWN // BLK), None, ALU.is_ge))
            for b in range(2, CHUNKS):
                link(stt(col_f[:], blk_f[0:1, :], float(OWN // BLK * b), col_f[:], ALU.is_ge, ALU.add))
            link(ts(col_f[:], col_f[:], float(BANK - OWN), None, ALU.mult))
            link(stt(col_tab[:, :, 0:HALF], halves, float(BLK), col_f[:].rearrange("p (i k) -> p i k", k=HALF),
                     ALU.mult, ALU.add))
            dve.wait_ge(s_winb, 2)
            link(nc.vector.tensor_reduce(narrow_f[:, 0:1], ps[0:1, 1, 0:NQ], AX.X, ALU.max))
            link(ts(narrow[:], narrow_f[:, 0:1], float(WIN), None, ALU.is_lt))
            dve.wait_ge(s_ld_w, 16 * 8)
            mark(tt(bgh[:, 0:2], bih_s[:, 0:2], bhh_s[:, 0:2], ALU.add))
            mark(cp(bgh[:, 2:3], bhh_s[:, 2:3]))
            w1v = w1_s[:, 0:D].rearrange("p (f o) -> p f o", o=OUT_F)
            for k in range(2):
                mark(tt(wa[:, k, :, :], w1v, a_s[:, k, :, :], ALU.mult))
            order.wait()
            for k in range(2):
                mark(nc.vector.tensor_reduce(w1_s[:, D + HEADS * k:D + HEADS * (k + 1)], wa[:, k, :, :], AX.X, ALU.add))
            order.wait()
            dve.wait_ge(s_ld_x, 32)
            norm(0)
            dve.wait_ge(s_relu, NT)
            nc.vector.memset(dlt[:, 0:1], 0.0).then_inc(s_h, CHUNKS)
            nc.vector.memset(dlt[:, 1:2], 0.0).then_inc(s_flag, 1)
            either(dve, program, order)


_INS = ["x", "src_t", "dst_t", "dst_rows", "attr_t", "ew_t", "we_t", "be", "wih_t", "whh_t", "bih", "bhh", "w1", "a1"]


def kernel(x, src, dst, edge_attr_4, edge_weight, L0_gnn_W_edge, L0_gnn_b_edge, L0_gnn_W_ih, L0_gnn_W_hh,
           L0_gnn_b_ih, L0_gnn_b_hh, L1_gnn_W, L1_gnn_a):
    import numpy as np
    import concourse.bacc as bacc
    from concourse.bass_utils import run_bass_kernel_spmd

    arr = [np.asarray(v) for v in (x, src, dst, edge_attr_4, edge_weight, L0_gnn_W_edge, L0_gnn_b_edge, L0_gnn_W_ih,
                                   L0_gnn_W_hh, L0_gnn_b_ih, L0_gnn_b_hh, L1_gnn_W, L1_gnn_a)]
    x, src, dst, attr, ew, we, be, wih, whh, bih, bhh, w1, a1 = arr
    pad = TILES * P - E
    src = np.concatenate([src, np.zeros(pad, src.dtype)])
    dst = np.concatenate([dst, np.full(pad, NP - 1, dst.dtype)])
    ew = np.concatenate([ew, np.zeros(pad, ew.dtype)])
    attr = np.concatenate([attr, np.zeros((pad, TYPES), attr.dtype)])
    data = {
        "x": x,
        "src_t": src.reshape(TILES, P).T,
        "dst_t": dst.reshape(TILES, P).T,
        "dst_rows": dst.reshape(4, NQ, P).transpose(1, 0, 2),
        "attr_t": attr.reshape(TILES, P, TYPES).transpose(1, 0, 2),
        "ew_t": ew.reshape(TILES, P).T,
        "we_t": we.reshape(TYPES * D, D).T,
        "be": be.reshape(TYPES * D),
        "wih_t": wih.T,
        "whh_t": whh.T,
        "bih": bih.reshape(3, D).T,
        "bhh": bhh.reshape(3, D).T,
        "w1": w1.transpose(1, 0, 2).reshape(D, HEADS * OUT_F),
        "a1": a1.reshape(HEADS, 2, OUT_F).transpose(1, 0, 2),
    }
    nc = bacc.Bacc("TRN2", target_bir_lowering=False, num_devices=1)
    arrays, args = {}, []
    for name in _INS:
        a = np.ascontiguousarray(data[name])
        arrays[f"in_{name}"] = a
        args.append(nc.dram_tensor(f"in_{name}", a.shape, mybir.dt.from_np(a.dtype), kind="ExternalInput").ap())
    args.append(nc.dram_tensor("out_0", (N, D), fp32, kind="ExternalOutput").ap())
    gnn_kernel(nc, *args)
    r = run_bass_kernel_spmd(nc, [arrays], core_ids=[0])
    return r.results[0]["out_0"]
```

```python
from contextlib import ExitStack

import concourse.bass as bass
from concourse import mybir

fp32 = mybir.dt.float32
bf16 = mybir.dt.bfloat16
i32 = mybir.dt.int32
ALU = mybir.AluOpType
ACT = mybir.ActivationFunctionType
AX = mybir.AxisListType

P = 128
N, E, D = 3125, 50000, 128
TYPES, STEPS = 4, 4
HEADS, OUT_F = 4, 32
SLOPE, LN_EPS, DEN_EPS = 0.2, 1e-5, 1e-16
WIN, BLK = 64, 32
BANK = 512
OWN = BANK - WIN
CHUNKS = -(-N // OWN)
NP = CHUNKS * OWN
NT = -(-NP // P)
ROWS = [min(P, NP - P * t) for t in range(NT)]
NBLK = NP // BLK
NWIN = NP // WIN
NG, HALF = 14, 14
G = 2 * HALF
TILES = NG * G
QT = HALF // 2
PAIRS = HALF // 2
LAG = 2
SLOTS = 4
X_TILES = (0, NT // 2, N // P)
RING = 5
SCORES = HALF * HEADS
BIG = 2.0 ** 100
REGS = 16
NQ = TILES // 4
assert NG * G >= -(-E // P) and NQ <= P and NP >= N


class Order:

    def __init__(self, eng, sem):
        self.eng, self.sem, self.n, self.loops = eng, sem, 0, 0

    def mark(self, ins):
        ins.then_inc(self.sem, 1)
        self.n += 1

    def wait(self):
        self.eng.wait_ge(self.sem, self.loops + self.n)

    def link(self, ins):
        self.mark(ins)
        self.wait()

    def enter(self, i, per):
        was = (self.loops, self.n, per)
        self.loops = self.loops + i * per
        return was

    def leave(self, was, count):
        loops, n, per = was
        assert self.n - n == per, (self.n - n, per)
        self.loops, self.n = loops, n + per * count


def gnn_kernel(nc, x, src_t, dst_t, dst_rows, attr_t, ew_t, we_t, be, wih_t, whh_t, bih, bhh, w1, a1, out,
               force_rounds=None):
    ctx = ExitStack()
    with ctx:
        def sb(name, shape, dt=fp32):
            return ctx.enter_context(nc.sbuf_tensor(name, shape, dt))

        def sem(name):
            return ctx.enter_context(nc.semaphore(name))

        tab0 = nc.dram_tensor("tab0", (NP * TYPES, D), fp32, kind="Internal").ap()
        tab1 = nc.dram_tensor("tab1", (NP, D), fp32, kind="Internal").ap()
        tab_s = nc.dram_tensor("tab_s", (NP, 2 * HEADS), fp32, kind="Internal").ap()

        src_i = sb("src_i", [P, TILES + G], i32)
        dst_i = sb("dst_i", [P, TILES], i32)
        rows_i = sb("rows_i", [NQ, 4, P], i32)
        attr = sb("attr", [P, TILES, TYPES])
        ew = sb("ew", [P, TILES])
        src_f = sb("src_f", [P, TILES])
        dst_f = sb("dst_f", [P, TILES])
        rel = sb("rel", [P, TILES])
        idx0 = sb("idx0", [P, TILES], i32)
        etype = sb("etype", [P, TILES])
        tmp_e = sb("tmp_e", [P, TILES])
        rows_f = sb("rows_f", [NQ, 4, P])
        dmin = sb("dmin", [NQ, 4])
        dmax = sb("dmax", [NQ, 4])
        win_i = sb("win_i", [NQ, 4], i32)
        win_f = sb("win_f", [NQ, 4])
        over = sb("over", [NQ, 5])
        blk_f = sb("blk_f", [P, TILES])
        col_f = sb("col_f", [1, TILES])
        col_tab = sb("col_tab", [1, 2 * NG, REGS], i32)
        blk_tab = sb("blk_tab", [1, 2 * NG, REGS], i32)
        narrow_f = sb("narrow_f", [1, 2])
        narrow = sb("narrow", [1, 1], i32)
        ident = sb("ident", [P, P])
        ident4 = sb("ident4", [P, 4, P], bf16)
        iota_i = sb("iota_i", [P, WIN], i32)
        iota = sb("iota", [P, WIN])
        start_i = sb("start_i", [P, NWIN], i32)
        start_f = sb("start_f", [P, NWIN])
        start_col = sb("start_col", [1, NWIN], i32)
        zeros = sb("zeros", [P, BANK], bf16)
        eps = sb("eps", [P, 1])
        neg_big = sb("neg_big", [P, 1])
        one = sb("one", [P, 1])
        xs = sb("xs", [P, NT, D])
        nrm = sb("nrm", [P, NT, D])
        stats = sb("stats", [P, NT, 6])
        mv = sb("mv", [P, NT, 2])
        rstd = sb("rstd", [P, NT])
        h_t = sb("h_t", [P, NP])
        agg_t = sb("agg_t", [P, NP])
        spill = sb("spill", [P, CHUNKS, WIN])
        gh = sb("gh", [P, 3, NP])
        over_gh = gh[:, :, :].rearrange("p g n -> p (g n)")
        n_pick, n_wmsg, n_hot_t = PAIRS * HEADS * P // 2, G * D, PAIRS * P
        pick = over_gh[0:2 * SCORES, 0:n_pick].bitcast(bf16).rearrange("p (j f b n) -> p j f b n", j=PAIRS, f=HEADS, b=2)
        wmsg = over_gh[:, n_pick:n_pick + n_wmsg].rearrange("p (k d) -> p k d", d=D)
        hot_t = over_gh[:, n_pick + n_wmsg:n_pick + n_wmsg + n_hot_t // 2].bitcast(bf16).rearrange("p (j e) -> p j e", e=P)
        n_to = n_pick + n_wmsg + n_hot_t // 2
        logits = over_gh[:, n_to:n_to + TILES * HEADS].rearrange("p (k f) -> p k f", f=HEADS)
        n_to += TILES * HEADS
        sh = over_gh[0:BLK, n_to:n_to + 3 * NBLK * HEADS].rearrange("p (q c f) -> p q c f", q=3, f=HEADS)
        n_to += 3 * NBLK * HEADS
        t_rest = over_gh[0:BLK, n_to:n_to + NBLK * HEADS]
        rz = sb("rz", [P, 3, 2, OWN])
        cand = sb("cand", [P, 2, OWN])
        dlt = sb("dlt", [P, OWN])
        we_s = sb("we_s", [P, TYPES * D])
        be_s = sb("be_s", [P, TYPES * D])
        be3 = sb("be3", [3 * BLK, TYPES * D], bf16)
        sel = sb("sel", [3 * BLK, P], bf16)
        wih_s = sb("wih_s", [P, 3 * D])
        whh_s = sb("whh_s", [P, 3 * D])
        bih_s = sb("bih_s", [P, 3])
        bhh_s = sb("bhh_s", [P, 3])
        bgh = sb("bgh", [P, 3])
        scores = sb("scores", [P, NT, 2 * HEADS])
        w1_s = sb("w1_s", [P, D + 2 * HEADS])
        a_s = sb("a_s", [P, 2, HEADS, OUT_F])
        wa = sb("wa", [P, 2, HEADS, OUT_F])
        stage = [sb(f"stage{h}", [P, HALF], i32) for h in range(2)]
        msg = sb("msg", [P, G, D])
        srow = sb("srow", [P, G, 2 * HEADS])
        hot = sb("hot", [P, G, WIN])
        neg = sb("neg", [P, G, WIN], bf16)
        rel_w = sb("rel_w", [P, G])
        tabst = sb("tabst", [P, SLOTS, TYPES * D])
        scr = sb("scr", [P, HALF, HEADS])
        lgt = sb("lgt", [P, HALF, HEADS])
        look = sb("look", [P, HALF, HEADS])
        etg = sb("etg", [P, HALF, HEADS])
        parts = sb("parts", [P, 3, SCORES], bf16)
        part12_t = sb("part12_t", [2 * SCORES, P], bf16)
        part3_t = sb("part3_t", [SCORES, P], bf16)
        ex = sb("ex", [P, G, HEADS])
        pmax = sb("pmax", [P, PAIRS, HEADS])
        m_acc = sb("m_acc", [P, NBLK * HEADS])
        d_acc = sb("d_acc", [P, NBLK * HEADS])
        look_a = sb("look_a", [P, 3, NBLK * HEADS], bf16)
        look_b = sb("look_b", [P, 3, NBLK * HEADS], bf16)
        t_part = sb("t_part", [BLK, 3, NBLK * HEADS], bf16)
        t32 = sb("t32", [BLK, NBLK, HEADS])
        den = sb("den", [P, NT, HEADS])

        ps = ctx.enter_context(nc.psum_tensor("ps", [P, 8, BANK], fp32))
        acc = ps[:, :, :].rearrange("p b c -> p (b c)")
        hot_ps = ps[:, 7, 0:n_hot_t // 2].bitcast(bf16).rearrange("p (j e) -> p j e", e=P)
        etg_ps = ps[:, RING, 0:3 * SCORES]
        part_ps = ps[:, RING + 1, 0:P].bitcast(bf16).rearrange("p (b e) -> p b e", e=P)
        max_ps = ps[:, 7, 0:3 * SCORES]
        den_ps = ps[:, 7, 3 * SCORES:3 * SCORES + PAIRS * HEADS]

        rows_loaded = sem("rows_loaded")
        table_weights_loaded = sem("table_weights_loaded")
        edges_loaded = sem("edges_loaded")
        weights_loaded = sem("weights_loaded")
        x_loaded = [sem(f"x_loaded{i}") for i in range(3)]
        bias_split = sem("bias_split")
        pool_order = sem("pool_order")
        consts_ready = sem("consts_ready")
        dve_order = sem("dve_order")
        windows_found = sem("windows_found")
        windows_spread = sem("windows_spread")
        flag_ready = sem("flag_ready")
        node_rows_turned = sem("node_rows_turned")
        h_added = sem("h_added")
        variances_ready = sem("variances_ready")
        deviations_ready = sem("deviations_ready")
        rows_normed = sem("rows_normed")
        normed_turned = sem("normed_turned")
        relu_done = sem("relu_done")
        h_ready = sem("h_ready")
        table_made = sem("table_made")
        table_moved = sem("table_moved")
        table_written = [sem(f"table_written{i}") for i in range(SLOTS)]
        gh_made = sem("gh_made")
        gh_moved = sem("gh_moved")
        rows_arrived = [sem(f"rows_arrived{q}") for q in range(4)]
        indices_staged = [sem(f"indices_staged{h}") for h in range(2)]
        hot_built = [sem(f"hot_built{h}") for h in range(2)]
        half_used = [sem(f"half_used{h}") for h in range(2)]
        sums_closed = sem("sums_closed")
        sums_moved = sem("sums_moved")
        overlap_added = sem("overlap_added")
        gi_made = sem("gi_made")
        gates_added = sem("gates_added")
        gates_ready = sem("gates_ready")
        cand_added = sem("cand_added")
        cand_ready = sem("cand_ready")
        layer_made = sem("layer_made")
        layer_moved = sem("layer_moved")
        scores_written = sem("scores_written")
        layer_written = sem("layer_written")
        t32_loaded = sem("t32_loaded")
        look_ready = sem("look_ready")
        masks_built = sem("masks_built")
        masks_turned = sem("masks_turned")
        hot_t_ready = sem("hot_t_ready")
        values_looked_up = sem("values_looked_up")
        logits_split = sem("logits_split")
        logits_turned = sem("logits_turned")
        parts_t_ready = sem("parts_t_ready")
        pair_spread = sem("pair_spread")
        pair_maxima_taken = sem("pair_maxima_taken")
        logits_shifted = sem("logits_shifted")
        exp_done = sem("exp_done")
        rows_weighted = sem("rows_weighted")
        window_dens_made = sem("window_dens_made")
        tile_finished = sem("tile_finished")
        out_written = sem("out_written")

        block = ctx.enter_context(nc.Block())

        def chunk_of(t):
            return (P * t + ROWS[t] - 1) // OWN

        def rounds_loop(eng, rounds, body):
            if rounds == 1:
                body(0)
            else:
                with eng.Fori(0, rounds, 1) as w:
                    body(w)

        def places(eng, table, g, h, top):
            loaded = nc.values_load_multi_w_load_instructions(
                table[0:1, bass.ds(g * 2 + h, 1), :].rearrange("p a b -> p (a b)"), engines=[eng.engine],
                min_val=0, max_val=top,
                skip_runtime_bounds_check_because="they follow from the targets, which are nodes")[1]
            return loaded[0:HALF]

        def evacuated(eng, k, t):
            eng.wait_ge(table_moved, k * NT + t + 1)

        def slot_free(eng, k, t):
            if t >= SLOTS:
                eng.wait_ge(table_written[t % SLOTS], k * (16 * tab_uses[t % SLOTS]) + 16 * (t // SLOTS))

        def tiles_of(c):
            return [t for t in range(NT) if chunk_of(t) == c]

        def either(eng, program, order=None):
            eng.wait_ge(flag_ready, 1)
            before = order.n if order else 0
            if force_rounds:
                return program(force_rounds)
            flag = eng.value_load(narrow[0:1, 0:1], min_val=0, max_val=1)
            with eng.If(flag):
                program(1)
            with eng.Else():
                if order:
                    order.n = before
                program(NWIN)

        def sweep(eng, rounds, ahead, both, alone, order=None, per=0, per_half=0, close=None):
            if rounds > 1:
                with eng.Fori(0, NG, 1) as g:
                    was_g = order.enter(g, 2 * (rounds * per + per_half)) if order else None
                    for h in range(2):
                        with eng.Fori(0, rounds, 1) as w:
                            was = order.enter(w, per) if order else None
                            alone(g, h, w)
                            if order:
                                order.leave(was, rounds)
                        if close:
                            close(g, h)
                    if order:
                        order.leave(was_g, NG)
                return
            ahead(0, 0)
            with eng.Fori(0, NG - 1, 1) as g:
                was_g = order.enter(g, 2 * per) if order else None
                both((g, 0), (g, 1))
                both((g, 1), (g + 1, 0))
                if order:
                    order.leave(was_g, NG - 1)
            both((NG - 1, 0), (NG - 1, 1))
            both((NG - 1, 1), None)

        def steps(eng, step, order=None, per=0):
            if STEPS > 1:
                with eng.Fori(0, STEPS - 1, 1) as st:
                    was = order.enter(st, per) if order else None
                    step(st, True)
                    if order:
                        order.leave(was, STEPS - 1)
            step(STEPS - 1, False)

        tab_uses = [len(range(i, NT, SLOTS)) for i in range(SLOTS)]

        @block.sync
        def _(sp):
            sp.dma_start(rows_i[:], dst_rows).then_inc(rows_loaded, 16)
            sp.dma_start(be_s[:], be.partition_broadcast(P)).then_inc(table_weights_loaded, 16)
            sp.dma_start(we_s[:], we_t).then_inc(table_weights_loaded, 16)
            for i in range(3):
                if i == 2:
                    sp.wait_ge(consts_ready, 1)
                    sp.dma_start(xs[0:N - X_TILES[2] * P, NT - 1, :], x[X_TILES[2] * P:N, :]).then_inc(x_loaded[2], 16)
                else:
                    t0, t1 = X_TILES[i], X_TILES[i + 1]
                    sp.dma_start(xs[:, t0:t1, :], x[t0 * P:t1 * P, :].rearrange("(t p) d -> p t d", p=P)).then_inc(x_loaded[i], 16)
            sp.dma_start(src_i[:, 0:TILES], src_t).then_inc(edges_loaded, 16)
            sp.dma_start(src_i[:, TILES:TILES + G], src_t[:, 0:G]).then_inc(edges_loaded, 16)
            sp.dma_start(dst_i[:], dst_t).then_inc(edges_loaded, 16)
            sp.dma_start(attr[:], attr_t).then_inc(edges_loaded, 16)
            sp.dma_start(ew[:], ew_t).then_inc(edges_loaded, 16)
            for dst, src in ((wih_s[:], wih_t), (whh_s[:], whh_t), (bih_s[:], bih), (bhh_s[:], bhh),
                             (w1_s[:, 0:D], w1), (a_s[:], a1.partition_broadcast(P))):
                sp.dma_start(dst, src).then_inc(weights_loaded, 16)
            def table(k):
                for t in range(NT):
                    evacuated(sp, k, t)
                    sp.dma_start(tab0[TYPES * P * t:TYPES * (P * t + ROWS[t]), :].rearrange("(p k) d -> p (k d)", k=TYPES),
                                 tabst[0:ROWS[t], t % SLOTS, :]).then_inc(table_written[t % SLOTS], 16)
            table(0)
            if STEPS > 1:
                with nc.sync.Fori(1, STEPS, 1) as k:
                    table(k)
            for t0, t1 in ((0, NT // 2), (NT // 2, NT - 1)):
                sp.wait_ge(layer_moved, t1)
                sp.dma_start(tab_s[P * t0:P * t1, :].rearrange("(t p) f -> p t f", p=P), scores[:, t0:t1, :]).then_inc(scores_written, 16)
            sp.wait_ge(layer_moved, NT)
            last = slice(P * (NT - 1), P * (NT - 1) + ROWS[NT - 1])
            sp.dma_start(tab_s[last, :], scores[0:ROWS[NT - 1], NT - 1, :]).then_inc(scores_written, 16)
            sp.wait_ge(scores_written, 48)
            sp.dma_start(t32[:], tab_s[:, HEADS:].rearrange("(c p) h -> p c h", p=BLK)).then_inc(t32_loaded, 16)
            sp.dma_start(tab1[0:P * (NT - 1), :].rearrange("(t p) d -> p t d", p=P), nrm[:, 0:NT - 1, :]).then_inc(layer_written, 16)
            sp.dma_start(tab1[last, :], nrm[0:ROWS[NT - 1], NT - 1, :]).then_inc(layer_written, 16)
            cuts = [(NT - 1) * i // 4 for i in range(5)]
            for t0, t1 in zip(cuts, cuts[1:]):
                sp.wait_ge(tile_finished, t1)
                sp.dma_start(out[P * t0:P * t1, :].rearrange("(t p) d -> p t d", p=P), nrm[:, t0:t1, :]).then_inc(out_written, 16)
            sp.wait_ge(tile_finished, NT)
            sp.dma_start(out[P * (NT - 1):N, :], nrm[0:N - P * (NT - 1), NT - 1, :]).then_inc(out_written, 16)
            sp.wait_ge(out_written, 16 * 5)

        @block.gpsimd
        def _(pool):
            pool.iota(iota_i[:], pattern=[[1, WIN]], base=0, channel_multiplier=0).then_inc(pool_order, 1)
            pool.iota(start_i[:], pattern=[[WIN, NWIN]], base=0, channel_multiplier=0).then_inc(pool_order, 1)
            pool.iota(start_col[:], pattern=[[BANK, CHUNKS], [WIN, OWN // WIN]], base=0,
                      channel_multiplier=0).then_inc(pool_order, 1)
            pool.memset(ident[:], 0.0).then_inc(pool_order, 1)
            pool.wait_ge(pool_order, 4)
            pool.affine_select(out=ident[:], in_=ident[:], compare_op=ALU.not_equal, fill=1.0, base=0,
                               pattern=[[-1, P]], channel_multiplier=1).then_inc(pool_order, 1)

            def wait_on(sem, value):
                value = pool.snap(value)
                pool.keepalive_nop([pool.lower_val_access(value)])
                pool.wait_ge(pool_order, 5)
                pool.wait_ge(sem, value)

            def gathers(n, table, to):
                for h in range(2):
                    wait_on(indices_staged[h], n + 1)
                    for k in range(HALF):
                        slot = h * HALF + k
                        pool.indirect_dma_start(to[:, slot, :], None, table,
                                                bass.IndirectOffsetOnAxis(stage[h][:, k:k + 1], 0)
                                                ).then_inc(rows_arrived[slot // QT], 16)

            with nc.gpsimd.Fori(0, STEPS, 1) as st:
                for i in range(SLOTS):
                    wait_on(table_written[i], (st + 1) * (16 * tab_uses[i]))
                with nc.gpsimd.Fori(0, NG, 1) as g:
                    gathers(st * NG + g, tab0, msg)
            pool.wait_ge(scores_written, 48)
            with nc.gpsimd.Fori(0, NG, 1) as g:
                gathers(g + STEPS * NG, tab_s, srow)
            pool.wait_ge(layer_written, 32)
            with nc.gpsimd.Fori(0, NG, 1) as g:
                gathers(g + (STEPS + 1) * NG, tab1, msg)

        @block.scalar
        def _(act):
            def norm(n, then):
                act.wait_ge(variances_ready, n + 1)
                act.activation(rstd[:], mv[:, :, 1], ACT.Sqrt, bias=eps[:, 0:1]).then_inc(deviations_ready, 1)
                for t in range(NT):
                    act.wait_ge(normed_turned, n * NT + t + 1)
                    act.activation(h_t[:, P * t:P * t + ROWS[t]], ps[:, 2 + t % 4, 0:ROWS[t]],
                                   ACT.Relu).then_inc(relu_done, 1)
                    if t >= 2:
                        then(t - 2)
                for t in range(NT - 2, NT):
                    then(t)

            def table_tile(k, t):
                act.wait_ge(table_made, k * NT + t + 1)
                slot_free(act, k, t)
                act.activation(tabst[0:ROWS[t], t % SLOTS, :], ps[0:ROWS[t], 6 + t % 2, :], ACT.Copy).then_inc(table_moved, 1)

            def sum_out(st):
                for c in range(CHUNKS):
                    act.wait_ge(sums_closed, st * CHUNKS + c + 1)
                    act.activation(agg_t[:, OWN * c:OWN * (c + 1)], ps[:, c, 0:OWN], ACT.Copy)
                    act.activation(spill[:, c, :], ps[:, c, OWN:BANK], ACT.Copy).then_inc(sums_moved, 1)

            def program(rounds):
                def step(st, more):
                    for m in range(3 * CHUNKS):
                        g, c = m % 3, m // 3
                        act.wait_ge(gh_made, st * (3 * CHUNKS) + m + 1)
                        act.activation(gh[:, g, OWN * c:OWN * (c + 1)], ps[:, m % 6, 0:OWN], ACT.Identity,
                                       bias=bgh[:, g:g + 1]).then_inc(gh_moved, 1)
                    sum_out(st)
                    for i in range(CHUNKS + LAG):
                        if 1 <= i <= CHUNKS:
                            act.wait_ge(cand_added, st * CHUNKS + i)
                            act.activation(cand[:, (i - 1) % 2, :], cand[:, (i - 1) % 2, :], ACT.Tanh,
                                           bias=bih_s[:, 2:3]).then_inc(cand_ready, 1)
                        if i < CHUNKS:
                            act.wait_ge(gates_added, st * CHUNKS + i + 1)
                            act.activation(rz[:, i % 3, :, :], rz[:, i % 3, :, :], ACT.Sigmoid).then_inc(gates_ready, 1)
                        if more and i >= LAG:
                            for t in tiles_of(i - LAG):
                                table_tile(st + 1, t)

                def rows_out(t):
                    act.wait_ge(layer_made, t + 1)
                    r = ROWS[t]
                    act.activation(nrm[0:r, t, :], ps[0:r, t % 2, 0:D], ACT.Copy)
                    act.activation(scores[0:r, t, :], ps[0:r, t % 2, D:D + 2 * HEADS], ACT.Copy).then_inc(layer_moved, 1)

                steps(nc.scalar, step)
                norm(1, rows_out)

                def start(n_hot, n, h):
                    act.wait_ge(hot_built[h], n_hot)
                    act.activation(neg[:, h * HALF:(h + 1) * HALF, :], hot[:, h * HALF:(h + 1) * HALF, :],
                                   ACT.Identity, scale=BIG, bias=neg_big[:, 0:1]).then_inc(masks_built, 1)
                    act.wait_ge(masks_turned, n + 1)
                    act.activation(hot_t[:], hot_ps, ACT.Identity, scale=1 / BIG, bias=one[:, 0:1]).then_inc(hot_t_ready, 1)

                def max_start(g, h, w):
                    start((g + STEPS * NG) * rounds + w + 1, (g * 2 + h) * rounds + w, h)

                def max_finish(g, h, w):
                    act.wait_ge(logits_turned, (g * 2 + h) * rounds + w + 1)
                    act.activation(part12_t[:], part_ps[0:2 * SCORES, 0, :], ACT.Copy)
                    act.activation(part3_t[:], part_ps[0:SCORES, 1, :], ACT.Copy).then_inc(parts_t_ready, 1)

                def sum_start(g, h, w):
                    start((g + (STEPS + 1) * NG) * rounds + w + 1, 2 * NG * rounds + (g * 2 + h) * rounds + w, h)

                def sum_finish(g, h, w):
                    act.wait_ge(logits_shifted, (g * 2 + h) * rounds + w + 1)
                    act.activation(ex[:, h * HALF:(h + 1) * HALF, :], lgt[:], ACT.Exp).then_inc(exp_done, 1)

                for start_half, finish_half in ((max_start, max_finish), (sum_start, sum_finish)):
                    def alone(g, h, w):
                        start_half(g, h, w)
                        finish_half(g, h, w)

                    sweep(nc.scalar, rounds, lambda g, h: alone(g, h, 0),
                          lambda now, after: after and alone(*after, 0), alone)
                sum_out(STEPS)

            act.wait_ge(consts_ready, 2)
            norm(0, lambda t: table_tile(0, t))
            either(act, program)

        @block.tensor
        def _(pe):
            mm = nc.tensor.matmul

            def norm(n, then):
                for t in range(NT):
                    pe.wait_ge(rows_normed, n * NT + t + 1)
                    if t >= 4:
                        pe.wait_ge(relu_done, n * NT + t - 3)
                    nc.tensor.transpose(ps[:, 2 + t % 4, 0:ROWS[t]], nrm[0:ROWS[t], t, :],
                                        ident[0:ROWS[t], 0:ROWS[t]]).then_inc(normed_turned, 1)
                    if t >= 2:
                        then(t - 2)
                for t in range(NT - 2, NT):
                    then(t)

            def table_tile(k, t):
                if isinstance(k, int) and k == 0:
                    pe.wait_ge(relu_done, t + 1)
                else:
                    pe.wait_ge(h_ready, k * CHUNKS + chunk_of(t) + 1)
                if t >= 2:
                    evacuated(pe, k, t - 2)
                at = ps[0:ROWS[t], 6 + t % 2, :]
                mm(at, h_t[:, P * t:P * t + ROWS[t]], we_s[:], start=True, stop=False)
                last = mm(at, sel[:, 0:ROWS[t]], be3[:], start=False, stop=True)
                last.then_inc(table_made, 1)

            def open_sums():
                for c in range(CHUNKS):
                    mm(ps[:, c, :], zeros[:, 0:P], zeros[:], start=True, stop=False)

            def close_sums():
                for c in range(CHUNKS):
                    mm(ps[:, c, :], zeros[:, 0:P], zeros[:], start=False, stop=True).then_inc(sums_closed, 1)

            def program(rounds):
                def columns(g, h, w):
                    top = CHUNKS * BANK - WIN
                    if rounds == 1:
                        return places(pe, col_tab, g, h, top)
                    return [pe.value_load(start_col[0:1, bass.ds(w, 1)], min_val=0, max_val=top)] * HALF

                def node_places(g, h, w):
                    if rounds == 1:
                        return places(pe, blk_tab, g, h, HEADS * (NBLK - 1))
                    return [w * (2 * HEADS)] * HALF

                def add_half(n, g, h):
                    def one(w):
                        cols = columns(g, h, w)
                        pe.wait_ge(hot_built[h], n * rounds + w + 1)
                        for k in range(HALF):
                            slot = h * HALF + k
                            if slot % QT == 0:
                                pe.wait_ge(rows_arrived[slot // QT], (n + 1) * (16 * QT))
                            last = mm(acc[:, bass.ds(cols[k], WIN)], msg[:, slot, 0:D], hot[:, slot, :], start=False, stop=False)
                        last.then_inc(half_used[h], 1)
                    rounds_loop(nc.tensor, rounds, one)

                def step(st, more):
                    for m in range(3 * CHUNKS):
                        g, c = m % 3, m // 3
                        if m >= 6:
                            pe.wait_ge(gh_moved, st * (3 * CHUNKS) + m - 5)
                        mm(ps[:, m % 6, 0:OWN], whh_s[:, D * g:D * (g + 1)], h_t[:, OWN * c:OWN * (c + 1)],
                           start=True, stop=True).then_inc(gh_made, 1)
                    pe.wait_ge(gh_moved, (st + 1) * (3 * CHUNKS))
                    evacuated(pe, st, NT - 1)
                    open_sums()
                    with nc.tensor.Fori(0, NG, 1) as g:
                        for h in range(2):
                            add_half(st * NG + g, g, h)
                    close_sums()
                    for i in range(CHUNKS + LAG):
                        if i < CHUNKS:
                            c = i
                            pe.wait_ge(sums_moved, st * CHUNKS + min(3 * (c + 1), CHUNKS))
                            if c >= 1:
                                pe.wait_ge(overlap_added, st * (CHUNKS - 1) + c)
                            if c >= 2:
                                pe.wait_ge(gates_added, st * CHUNKS + c - 1)
                            for g in range(3):
                                if g == 2 and c >= 2:
                                    pe.wait_ge(cand_added, st * CHUNKS + c - 1)
                                mm(ps[:, 3 * (c % 2) + g, 0:OWN], wih_s[:, D * g:D * (g + 1)],
                                   agg_t[:, OWN * c:OWN * (c + 1)], start=True, stop=True).then_inc(gi_made, 1)
                        if i >= LAG:
                            for t in tiles_of(i - LAG):
                                if more:
                                    table_tile(st + 1, t)
                                else:
                                    pe.wait_ge(h_ready, STEPS * CHUNKS + i - LAG + 1)
                                    if t >= 2:
                                        pe.wait_ge(h_added, t - 1)
                                    nc.tensor.transpose(ps[0:ROWS[t], 6 + t % 2, 0:P], h_t[:, P * t:P * t + ROWS[t]],
                                                        ident[:]).then_inc(node_rows_turned, 1)

                steps(nc.tensor, step)

                def layer_rows(t):
                    pe.wait_ge(relu_done, NT + t + 1)
                    if t >= 2:
                        pe.wait_ge(layer_moved, t - 1)
                    mm(ps[0:ROWS[t], t % 2, 0:D + 2 * HEADS], h_t[:, P * t:P * t + ROWS[t]], w1_s[:],
                       start=True, stop=True).then_inc(layer_made, 1)

                norm(1, layer_rows)
                pe.wait_ge(layer_moved, NT)

                def turn(n, h):
                    pe.wait_ge(masks_built, n + 1)
                    for j in range(PAIRS):
                        s0 = h * HALF + 2 * j
                        last = nc.tensor.transpose(hot_ps[:, j, :], neg[:, s0:s0 + 2, :].rearrange("p a b -> p (a b)"),
                                                   ident4[:, 0, :])
                    last.then_inc(masks_turned, 1)

                def look_up(n, where, at):
                    pe.wait_ge(hot_t_ready, n + 1)
                    for k in range(HALF):
                        last = mm(at[:, k * 3 * HEADS:(k + 1) * 3 * HEADS], hot_t[:, k // 2, :],
                                  (look_a, look_b)[k % 2][:, :, bass.ds(where[k], HEADS)], start=True, stop=True)
                    last.then_inc(values_looked_up, 1)

                def max_finish(g, h, w):
                    have = pe.snap((g * 2 + h) * rounds + w + 1)
                    pe.wait_ge(look_ready, 1)
                    pe.wait_ge(logits_split, have)
                    nc.tensor.transpose(part_ps[0:2 * SCORES, 0, :], parts[:, 0:2, :].rearrange("p a b -> p (a b)"), ident4[:, 0, :])
                    nc.tensor.transpose(part_ps[0:SCORES, 1, :], parts[:, 2, :], ident4[:, 0, :]).then_inc(logits_turned, 1)

                def spread(n, h, js):
                    if js.start == 0:
                        pe.wait_ge(parts_t_ready, n + 1)
                        pe.wait_ge(pair_maxima_taken, n * PAIRS + 1)
                    for j in js:
                        bank = ps[:, j % RING, :]
                        if j >= RING:
                            pe.wait_ge(pair_maxima_taken, n * PAIRS + j - RING + 2)
                        s0 = h * HALF + 2 * j
                        mm(bank, neg[:, s0:s0 + 2, :].rearrange("p a b -> p (a b)"),
                           ident4[:].rearrange("p a b -> p (a b)"), start=True, stop=False)
                        for hd in range(HEADS):
                            at = bank[:, P * hd:P * (hd + 1)]
                            rows = pick[:, j, hd, :, :].rearrange("p a b -> p (a b)")
                            mm(at, rows, part12_t[:], start=False, stop=False)
                            last = mm(at, rows[0:SCORES, :], part3_t[:], start=False, stop=(hd == HEADS - 1))
                        last.then_inc(pair_spread, 1)

                pe.wait_ge(look_ready, 1)

                def max_alone(g, h, w):
                    n = (g * 2 + h) * rounds + w
                    where = node_places(g, h, w)
                    turn(n, h)
                    look_up(n, where, etg_ps)
                    max_finish(g, h, w)
                    spread(n, h, range(0, PAIRS))

                def max_ahead(g, h):
                    where = node_places(g, h, 0)
                    turn(g * 2 + h, h)
                    look_up(g * 2 + h, where, etg_ps)
                    max_finish(g, h, 0)

                def max_both(now, after):
                    n, h = now[0] * 2 + now[1], now[1]
                    if after:
                        n1 = after[0] * 2 + after[1]
                        where = node_places(*after, 0)
                    spread(n, h, range(0, 2))
                    if after:
                        turn(n1, after[1])
                    spread(n, h, range(2, 4))
                    if after:
                        look_up(n1, where, etg_ps)
                    spread(n, h, range(4, PAIRS))
                    if after:
                        max_finish(*after, 0)

                sweep(nc.tensor, rounds, max_ahead, max_both, max_alone)
                pe.wait_ge(look_ready, 2)
                open_sums()

                def sum_finish(g, h, w):
                    pe.wait_ge(exp_done, (g * 2 + h) * rounds + w + 1)
                    for k in range(HALF):
                        slot = h * HALF + k
                        lo = WIN * (k % 2)
                        last = mm(den_ps[lo:lo + WIN, HEADS * (k // 2):HEADS * (k // 2 + 1)], hot[:, slot, :], ex[:, slot, :],
                                  start=True, stop=True)
                    last.then_inc(window_dens_made, 1)

                def add_rows(n, h, cols, ks):
                    if ks.start == 0:
                        pe.wait_ge(rows_weighted, n + 1)
                    for k in ks:
                        slot = h * HALF + k
                        last = mm(acc[:, bass.ds(cols[k], WIN)], wmsg[:, slot, :], hot[:, slot, :], start=False, stop=False)
                    if ks.stop == HALF:
                        last.then_inc(half_used[h], 1)

                def sum_alone(g, h, w):
                    n = (g * 2 + h) * rounds + w
                    where = node_places(g, h, w)
                    turn(2 * NG * rounds + n, h)
                    look_up(2 * NG * rounds + n, where, max_ps)
                    sum_finish(g, h, w)
                    add_rows(n, h, columns(g, h, w), range(0, HALF))

                def sum_ahead(g, h):
                    n = 2 * NG + g * 2 + h
                    where = node_places(g, h, 0)
                    turn(n, h)
                    look_up(n, where, max_ps)
                    sum_finish(g, h, 0)

                def sum_both(now, after):
                    n, h = now[0] * 2 + now[1], now[1]
                    if after:
                        n1 = 2 * NG + after[0] * 2 + after[1]
                        where = node_places(*after, 0)
                        turn(n1, after[1])
                        look_up(n1, where, max_ps)
                    cols = columns(*now, 0)
                    add_rows(n, h, cols, range(0, HALF // 3))
                    if after:
                        sum_finish(*after, 0)
                    add_rows(n, h, cols, range(HALF // 3, HALF))

                sweep(nc.tensor, rounds, sum_ahead, sum_both, sum_alone)
                close_sums()
                pe.wait_ge(sums_moved, (STEPS + 1) * CHUNKS)
                for t in range(NT):
                    c = chunk_of(t)
                    if c >= 1:
                        pe.wait_ge(overlap_added, STEPS * (CHUNKS - 1) + c)
                    if t >= 4:
                        pe.wait_ge(tile_finished, t - 3)
                    nc.tensor.transpose(ps[0:ROWS[t], t % 4, 0:P], agg_t[:, P * t:P * t + ROWS[t]],
                                        ident[:]).then_inc(node_rows_turned, 1)

            pe.wait_ge(pool_order, 5)
            pe.wait_ge(consts_ready, 2)
            pe.wait_ge(windows_found, 1)
            for q in range(4):
                last = mm(ps[:, 0, NQ * q:NQ * (q + 1)], win_f[:, q:q + 1].to_broadcast([NQ, P]),
                          ident[0:NQ, 0:NQ], start=True, stop=True)
            last.then_inc(windows_spread, 1)
            nc.tensor.transpose(ps[0:1, 1, 0:NQ], over[:, 4:5], ident[0:NQ, 0:NQ]).then_inc(windows_spread, 1)
            pe.wait_ge(table_weights_loaded, 32)
            pe.wait_ge(bias_split, 1)
            norm(0, lambda t: table_tile(0, t))
            either(pe, program)

        @block.vector
        def _(dve):
            order = Order(dve, dve_order)
            link, mark = order.link, order.mark
            tt, ts, stt, cp = nc.vector.tensor_tensor, nc.vector.tensor_scalar, nc.vector.scalar_tensor_tensor, nc.vector.tensor_copy

            def stats_of(t):
                mark(nc.vector.bn_stats(stats[:, t, :], xs[:, t, :]))

            def norm(n):
                order.wait()
                for t in range(NT):
                    last = nc.vector.bn_aggr(mv[:, t, :], stats[:, t, :])
                last.then_inc(variances_ready, 1)
                dve.wait_ge(deviations_ready, n + 1)
                link(nc.vector.reciprocal(rstd[:], rstd[:]))
                for t in range(NT):
                    ts(nrm[:, t, :], xs[:, t, :], mv[:, t, 0:1], rstd[:, t:t + 1], ALU.subtract, ALU.mult).then_inc(rows_normed, 1)

            def overlaps(st):
                for c in range(1, CHUNKS):
                    dve.wait_ge(sums_moved, st * CHUNKS + c + 1)
                    tt(agg_t[:, OWN * c:OWN * c + WIN], agg_t[:, OWN * c:OWN * c + WIN], spill[:, c - 1, :],
                       ALU.add).then_inc(overlap_added, 1)

            def program(rounds):
                def acc_places(g, h, w):
                    if rounds == 1:
                        return places(dve, blk_tab, g, h, HEADS * (NBLK - 1))
                    return [w * (2 * HEADS)] * HALF

                def free_half(n, h, w):
                    dve.wait_ge(half_used[h], n * rounds + w + 1)

                def build_hot(n, g, h, w):
                    sl = slice(h * HALF, (h + 1) * HALF)
                    if rounds == 1:
                        r = rel[:, bass.ds(g * G + h * HALF, HALF)]
                    else:
                        link(ts(rel_w[:, sl], dst_f[:, bass.ds(g * G + h * HALF, HALF)], start_f[:, bass.ds(w, 1)], None,
                                ALU.subtract))
                        r = rel_w[:, sl]
                    tt(hot[:, sl, :], iota[:].unsqueeze(1).to_broadcast([P, HALF, WIN]),
                       r.unsqueeze(2).to_broadcast([P, HALF, WIN]), ALU.is_equal).then_inc(hot_built[h], 1)

                def stage_idx(n, g, h, idx):
                    cp(stage[h][:], idx[:, bass.ds(g * G + h * HALF, HALF)]).then_inc(indices_staged[h], 1)

                extra = 0 if rounds == 1 else 1

                def step(st, more):
                    with nc.vector.Fori(0, NG, 1) as g:
                        it = order.enter(g, extra * 2 * rounds)
                        for h in range(2):
                            n = st * NG + g
                            free_half(n, h, 0)
                            stage_idx(n, g, h, idx0)

                            def one(w):
                                was = order.enter(w, extra)
                                free_half(n, h, w)
                                build_hot(n, g, h, w)
                                order.leave(was, rounds)
                            rounds_loop(nc.vector, rounds, one)
                        order.leave(it, NG)
                    overlaps(st)
                    for i in range(CHUNKS + LAG):
                        if 1 <= i <= CHUNKS:
                            c = i - 1
                            dve.wait_ge(gates_ready, st * CHUNKS + c + 1)
                            if c >= 2:
                                dve.wait_ge(h_ready, (st + 1) * CHUNKS + c - 1)
                            link(tt(cand[:, c % 2, :], rz[:, c % 3, 0, :], gh[:, 2, OWN * c:OWN * (c + 1)], ALU.mult))
                            dve.wait_ge(gi_made, st * (3 * CHUNKS) + 3 * c + 3)
                            tt(cand[:, c % 2, :], cand[:, c % 2, :], ps[:, 3 * (c % 2) + 2, 0:OWN], ALU.add).then_inc(cand_added, 1)
                        if i < CHUNKS:
                            c = i
                            if c >= 3:
                                dve.wait_ge(h_ready, (st + 1) * CHUNKS + c - 2)
                            for g in range(2):
                                dve.wait_ge(gi_made, st * (3 * CHUNKS) + 3 * c + g + 1)
                                last = tt(rz[:, c % 3, g, :], ps[:, 3 * (c % 2) + g, 0:OWN], gh[:, g, OWN * c:OWN * (c + 1)], ALU.add)
                            last.then_inc(gates_added, 1)
                        if 1 <= i <= CHUNKS:
                            c = i - 1
                            own = slice(OWN * c, OWN * (c + 1))
                            dve.wait_ge(cand_ready, st * CHUNKS + c + 1)
                            if c >= 1:
                                dve.wait_ge(h_ready, (st + 1) * CHUNKS + c)
                            link(tt(dlt[:], h_t[:, own], cand[:, c % 2, :], ALU.subtract))
                            link(tt(dlt[:], dlt[:], rz[:, c % 3, 1, :], ALU.mult))
                            tt(h_t[:, own], cand[:, c % 2, :], dlt[:], ALU.add).then_inc(h_ready, 1)
                        if not more and i >= LAG:
                            for t in tiles_of(i - LAG):
                                dve.wait_ge(node_rows_turned, t + 1)
                                tt(xs[0:ROWS[t], t, :], xs[0:ROWS[t], t, :], ps[0:ROWS[t], 6 + t % 2, 0:P], ALU.add).then_inc(h_added, 1)
                                dve.wait_ge(h_added, t + 1)
                                stats_of(t)

                steps(nc.vector, step, order, extra * 2 * NG * rounds + 3 * CHUNKS)
                for h in range(2):
                    free_half(STEPS * NG, h, 0)
                    stage_idx(STEPS * NG, 0, h, src_i)
                norm(1)

                def place():
                    flat = t32[:].rearrange("p c f -> p (c f)")
                    split(t_part, flat, t_rest)
                    order.wait()
                    for table, p0 in ((look_a, 0), (look_b, 2 * BLK)):
                        cp(table[p0:p0 + BLK, :, :], t_part[:])
                        last = cp(table[p0 + BLK:p0 + 2 * BLK, :, 0:(NBLK - 1) * HEADS], t_part[:, :, HEADS:])
                    return last

                def split(into, value, rest):
                    link(cp(into[:, 0, :], value))
                    link(tt(rest, value, into[:, 0, :], ALU.subtract))
                    link(cp(into[:, 1, :], rest))
                    mark(tt(into[:, 2, :], rest, into[:, 1, :], ALU.subtract))

                def looked_up(at):
                    return nc.vector.tensor_reduce(look[:], at.rearrange("p (k a f) -> p k f a", a=3, f=HEADS), AX.X, ALU.add)

                def merge(table, op):
                    v = table[:].rearrange("p (c f) -> p c f", f=HEADS)
                    for q in range(3):
                        mark(cp(sh[:, q, :, :], v[BLK * (q + 1):BLK * (q + 2), :, :]))
                    order.wait()
                    link(tt(t32[:], v[0:BLK, :, :], sh[:, 1, :, :], op))
                    link(tt(t32[:, 1:, :], t32[:, 1:, :], sh[:, 0, 0:NBLK - 1, :], op))
                    link(tt(t32[:, 1:, :], t32[:, 1:, :], sh[:, 2, 0:NBLK - 1, :], op))

                first, second = (ident[0:2 * SCORES, SCORES * i:SCORES * (i + 1)].rearrange("p (j b f) -> p j b f", b=2, f=HEADS)
                                 for i in range(2))
                for b in range(2):
                    for j in range(PAIRS):
                        last = tt(pick[:, j, :, b, :], first[:, j, b, :].unsqueeze(2).to_broadcast([2 * SCORES, HEADS, WIN]),
                                  second[:, j, b, :].unsqueeze(2).to_broadcast([2 * SCORES, HEADS, WIN]), ALU.add)
                mark(last)
                dve.wait_ge(t32_loaded, 16)
                place().then_inc(look_ready, 1)

                def logits_of(to, g, h, target):
                    link(tt(scr[:], target, srow[:, h * HALF:(h + 1) * HALF, 0:HEADS], ALU.add))
                    link(stt(lgt[:], scr[:], SLOPE, scr[:], ALU.mult, ALU.max))
                    return tt(to, lgt[:], ew[:, bass.ds(g * G + h * HALF, HALF)].unsqueeze(2).to_broadcast([P, HALF, HEADS]), ALU.mult)

                def stored(g, h):
                    return logits[:, bass.ds(g * G + h * HALF, HALF), :]

                def scatter(table, part, where, j, op):
                    order.wait()
                    for b in range(2):
                        lo = WIN * b
                        at = table[lo:lo + WIN, bass.ds(where[2 * j + b], HEADS)]
                        last = tt(at, at, part[lo:lo + WIN, :], op)
                    mark(last)

                def max_start(g, h, w):
                    build_hot(g + STEPS * NG, g, h, w)

                def next_rows(g, h, n):
                    stage_idx(n + 1, g + 1, h, src_i)

                def max_finish(g, h, w):
                    n = (g * 2 + h) * rounds + w
                    for q in (2 * h, 2 * h + 1):
                        dve.wait_ge(rows_arrived[q], (g + STEPS * NG + 1) * (16 * QT))
                    dve.wait_ge(values_looked_up, n + 1)
                    link(looked_up(etg_ps))
                    if rounds > 1:
                        mark(tt(etg[:], etg[:], look[:], ALU.add))
                    link(logits_of(lgt[:], g, h, look[:]))
                    if rounds == 1:
                        cp(stored(g, h), lgt[:])
                    flat, rest = (v[:].rearrange("p k f -> p (k f)") for v in (lgt, scr))
                    link(cp(parts[:, 0, :], flat))
                    link(tt(rest, flat, parts[:, 0, :], ALU.subtract))
                    link(cp(parts[:, 1, :], rest))
                    tt(parts[:, 2, :], rest, parts[:, 1, :], ALU.subtract).then_inc(logits_split, 1)
                    if rounds == 1:
                        next_rows(g, h, g + STEPS * NG)

                def max_half(g, h):
                    order.wait()
                    link(logits_of(lgt[:], g, h, etg[:]))
                    mark(cp(stored(g, h), lgt[:]))
                    link(nc.vector.memset(etg[:], 0.0))
                    next_rows(g, h, g + STEPS * NG)

                def take_max(g, h, w, where, js):
                    n = (g * 2 + h) * rounds + w
                    for j in range(js.start, js.stop + 1):
                        if j < js.stop:
                            dve.wait_ge(pair_spread, n * PAIRS + j + 1)
                            nc.vector.tensor_reduce(pmax[:, j, :], ps[:, j % RING, :].rearrange("p (f e) -> p f e", e=P),
                                                    AX.X, ALU.max).then_inc(pair_maxima_taken, 1)
                        if j > js.start:
                            dve.wait_ge(pair_maxima_taken, n * PAIRS + j + 1)
                            scatter(m_acc, pmax[:, j - 1, :], where, j - 1, ALU.max)

                def max_ahead(g, h):
                    max_start(g, h, 0)
                    max_finish(g, h, 0)

                def max_both(now, after):
                    if after:
                        max_start(*after, 0)
                    where = acc_places(*now, 0)
                    take_max(*now, 0, where, range(0, RING))
                    if after:
                        max_finish(*after, 0)
                    take_max(*now, 0, where, range(RING, PAIRS))

                def max_alone(g, h, w):
                    max_start(g, h, w)
                    max_finish(g, h, w)
                    take_max(g, h, w, acc_places(g, h, w), range(0, PAIRS))

                links = extra + (1 if rounds > 1 else 0)
                sweep(nc.vector, rounds, max_ahead, max_both, max_alone, order, links + 7 + PAIRS, 5, max_half)
                order.wait()
                merge(m_acc, ALU.max)
                place().then_inc(look_ready, 1)

                def sum_start(g, h, w):
                    free_half(g + STEPS * NG, h, w)
                    build_hot(g + (STEPS + 1) * NG, g, h, w)

                def sum_finish(g, h, w):
                    n = (g * 2 + h) * rounds + w
                    where = acc_places(g, h, w)
                    dve.wait_ge(values_looked_up, 2 * NG * rounds + n + 1)
                    link(looked_up(max_ps))
                    link(tt(lgt[:], stored(g, h), look[:], ALU.subtract))
                    ts(lgt[:], lgt[:], 0.0, None, ALU.min).then_inc(logits_shifted, 1)
                    dve.wait_ge(window_dens_made, n + 1)
                    for j in range(PAIRS):
                        scatter(d_acc, den_ps[:, HEADS * j:HEADS * (j + 1)], where, j, ALU.add)

                def sum_work(g, h, w):
                    n = (g * 2 + h) * rounds + w
                    sl = slice(h * HALF, (h + 1) * HALF)
                    for q in (2 * h, 2 * h + 1):
                        dve.wait_ge(rows_arrived[q], (g + (STEPS + 1) * NG + 1) * (16 * QT))
                    dve.wait_ge(exp_done, n + 1)
                    tt(wmsg[:, sl, :].rearrange("p k (f o) -> p k f o", o=OUT_F), msg[:, sl, :].rearrange("p k (f o) -> p k f o", o=OUT_F),
                       ex[:, sl, :].unsqueeze(3).to_broadcast([P, HALF, HEADS, OUT_F]), ALU.mult).then_inc(rows_weighted, 1)
                    if rounds == 1:
                        next_rows(g, h, g + (STEPS + 1) * NG)

                def sum_half(g, h):
                    next_rows(g, h, g + (STEPS + 1) * NG)

                def sum_ahead(g, h):
                    sum_start(g, h, 0)
                    sum_finish(g, h, 0)

                def sum_both(now, after):
                    if after:
                        sum_start(*after, 0)
                    sum_work(*now, 0)
                    if after:
                        sum_finish(*after, 0)

                def sum_alone(g, h, w):
                    sum_start(g, h, w)
                    sum_finish(g, h, w)
                    sum_work(g, h, w)

                sweep(nc.vector, rounds, sum_ahead, sum_both, sum_alone, order, extra + 2 + PAIRS, 0, sum_half)
                order.wait()
                merge(d_acc, ALU.add)
                per = P // BLK
                for q in range(per):
                    have = len(range(q, NBLK, per))
                    mark(cp(den[BLK * q:BLK * (q + 1), 0:have, :], t32[:, q::per, :]))
                order.wait()
                link(ts(den[:], den[:], DEN_EPS, None, ALU.add))
                link(nc.vector.reciprocal(den[:], den[:]))
                overlaps(STEPS)
                for t in range(NT):
                    r = ROWS[t]
                    dve.wait_ge(node_rows_turned, NT + t + 1)
                    link(tt(nrm[0:r, t, :].rearrange("p (f o) -> p f o", o=OUT_F),
                            ps[0:r, t % 4, 0:P].rearrange("p (f o) -> p f o", o=OUT_F),
                            den[0:r, t, :].unsqueeze(2).to_broadcast([r, HEADS, OUT_F]), ALU.mult))
                    tt(nrm[0:r, t, :], nrm[0:r, t, :], xs[0:r, t, :], ALU.add).then_inc(tile_finished, 1)

            mark(nc.vector.memset(xs[:, NT - 1, :], 0.0))
            order.wait()
            nc.vector.memset(eps[:], LN_EPS).then_inc(consts_ready, 1)
            nc.vector.memset(neg_big[:], -BIG)
            nc.vector.memset(one[:], 1.0).then_inc(pair_maxima_taken, 1)
            nc.vector.memset(etg[:], 0.0)
            nc.vector.memset(col_tab[:], 0)
            link(nc.vector.memset(blk_tab[:], 0))
            link(nc.vector.memset(sel[:], 0.0))
            for k in range(3):
                nc.vector.memset(sel[BLK * k:BLK * k + 1, :], 1.0)
            nc.vector.memset(zeros[:], 0.0)
            nc.vector.memset(look_a[:], 0.0)
            nc.vector.memset(look_b[:], 0.0)
            nc.vector.memset(d_acc[:], 0.0)
            nc.vector.memset(den[:], 1.0)
            nc.vector.memset(m_acc[:], -BIG)
            nc.vector.memset(over[:], 0.0).then_inc(half_used[0], 1)
            nc.vector.memset(scr[:, 0, 0:1], 0.0).then_inc(half_used[1], 1)
            dve.wait_ge(pool_order, 5)
            for k in range(4):
                cp(ident4[:, k, :], ident[:])
            cp(start_f[:], start_i[:])
            mark(cp(iota[:], iota_i[:]))
            order.wait()
            nc.vector.memset(scr[:, 0, 1:2], 0.0).then_inc(consts_ready, 1)
            dve.wait_ge(rows_loaded, 16)
            link(cp(rows_f[:], rows_i[:]))
            mark(nc.vector.tensor_reduce(dmax[:], rows_f[:], AX.X, ALU.max))
            link(nc.vector.tensor_reduce(dmin[:], rows_f[:], AX.X, ALU.min))
            link(cp(win_i[:], dmin[:]))
            link(ts(win_i[:], win_i[:], 5, None, ALU.arith_shift_right))
            mark(cp(win_f[:], win_i[:]))
            order.wait()
            link(stt(over[:, 0:4], win_f[:], -float(BLK), dmax[:], ALU.mult, ALU.add))
            nc.vector.tensor_reduce(over[:, 4:5], over[:, 0:4], AX.X, ALU.max).then_inc(windows_found, 1)
            dve.wait_ge(table_weights_loaded, 32)
            bias, rest = be_s[0:3 * BLK, :], rz[0:3 * BLK, :, :, :].rearrange("p a b c -> p (a b c)")[:, 0:TYPES * D]
            rough = neg[0:3 * BLK, :, :].rearrange("p a b -> p (a b)")[:, 0:TYPES * D]
            link(cp(rough, bias))
            mark(cp(be3[0:BLK, :], rough[0:BLK, :]))
            link(tt(rest, bias, rough, ALU.subtract))
            link(cp(rough, rest))
            mark(cp(be3[BLK:2 * BLK, :], rough[BLK:2 * BLK, :]))
            tt(be3[2 * BLK:, :], rest[2 * BLK:, :], rough[2 * BLK:, :], ALU.subtract).then_inc(bias_split, 1)
            for i in range(3):
                dve.wait_ge(x_loaded[i], 16)
                for t in range(X_TILES[i], (X_TILES + (NT,))[i + 1]):
                    stats_of(t)
            norm(0)
            dve.wait_ge(edges_loaded, 80)
            mark(cp(dst_f[:], dst_i[:]))
            mark(cp(src_f[:], src_i[:, 0:TILES]))
            link(nc.vector.tensor_reduce(tmp_e[:], attr[:], AX.X, ALU.max))
            mark(tt(etype[:], attr[:, :, 2], tmp_e[:], ALU.is_lt))
            mark(tt(rel[:], attr[:, :, 1], tmp_e[:], ALU.is_lt))
            link(tt(tmp_e[:], attr[:, :, 0], tmp_e[:], ALU.is_lt))
            link(stt(etype[:], etype[:], 1.0, rel[:], ALU.add, ALU.mult))
            link(stt(etype[:], etype[:], 1.0, tmp_e[:], ALU.add, ALU.mult))
            link(stt(idx0[:], src_f[:], float(TYPES), etype[:], ALU.mult, ALU.add))
            dve.wait_ge(windows_spread, 1)
            link(cp(blk_f[:], ps[:, 0, 0:TILES]))
            mark(stt(rel[:], blk_f[:], -float(BLK), dst_f[:], ALU.mult, ALU.add))
            halves = blk_f[0:1, :].rearrange("p (i k) -> p i k", k=HALF)
            mark(ts(blk_tab[:, :, 0:HALF], halves, float(HEADS), None, ALU.mult))
            link(ts(col_f[:], blk_f[0:1, :], float(OWN // BLK), None, ALU.is_ge))
            for b in range(2, CHUNKS):
                link(stt(col_f[:], blk_f[0:1, :], float(OWN // BLK * b), col_f[:], ALU.is_ge, ALU.add))
            link(ts(col_f[:], col_f[:], float(BANK - OWN), None, ALU.mult))
            link(stt(col_tab[:, :, 0:HALF], halves, float(BLK), col_f[:].rearrange("p (i k) -> p i k", k=HALF),
                     ALU.mult, ALU.add))
            dve.wait_ge(windows_spread, 2)
            link(nc.vector.tensor_reduce(narrow_f[:, 0:1], ps[0:1, 1, 0:NQ], AX.X, ALU.max))
            link(ts(narrow[:], narrow_f[:, 0:1], float(WIN), None, ALU.is_lt))
            dve.wait_ge(weights_loaded, 16 * 6)
            mark(tt(bgh[:, 0:2], bih_s[:, 0:2], bhh_s[:, 0:2], ALU.add))
            mark(cp(bgh[:, 2:3], bhh_s[:, 2:3]))
            w1v = w1_s[:, 0:D].rearrange("p (f o) -> p f o", o=OUT_F)
            for k in range(2):
                mark(tt(wa[:, k, :, :], w1v, a_s[:, k, :, :], ALU.mult))
            order.wait()
            for k in range(2):
                mark(nc.vector.tensor_reduce(w1_s[:, D + HEADS * k:D + HEADS * (k + 1)], wa[:, k, :, :], AX.X, ALU.add))
            order.wait()
            dve.wait_ge(relu_done, NT)
            nc.vector.memset(dlt[:, 0:1], 0.0).then_inc(h_ready, CHUNKS)
            nc.vector.memset(dlt[:, 1:2], 0.0).then_inc(flag_ready, 1)
            either(dve, program, order)


_INS = ["x", "src_t", "dst_t", "dst_rows", "attr_t", "ew_t", "we_t", "be", "wih_t", "whh_t", "bih", "bhh", "w1", "a1"]


def kernel(x, src, dst, edge_attr_4, edge_weight, L0_gnn_W_edge, L0_gnn_b_edge, L0_gnn_W_ih, L0_gnn_W_hh,
           L0_gnn_b_ih, L0_gnn_b_hh, L1_gnn_W, L1_gnn_a):
    import numpy as np
    import concourse.bacc as bacc
    from concourse.bass_utils import run_bass_kernel_spmd

    arr = [np.asarray(v) for v in (x, src, dst, edge_attr_4, edge_weight, L0_gnn_W_edge, L0_gnn_b_edge, L0_gnn_W_ih,
                                   L0_gnn_W_hh, L0_gnn_b_ih, L0_gnn_b_hh, L1_gnn_W, L1_gnn_a)]
    x, src, dst, attr, ew, we, be, wih, whh, bih, bhh, w1, a1 = arr
    pad = TILES * P - E
    src = np.concatenate([src, np.zeros(pad, src.dtype)])
    dst = np.concatenate([dst, np.full(pad, NP - 1, dst.dtype)])
    ew = np.concatenate([ew, np.zeros(pad, ew.dtype)])
    attr = np.concatenate([attr, np.zeros((pad, TYPES), attr.dtype)])
    data = {
        "x": x,
        "src_t": src.reshape(TILES, P).T,
        "dst_t": dst.reshape(TILES, P).T,
        "dst_rows": dst.reshape(4, NQ, P).transpose(1, 0, 2),
        "attr_t": attr.reshape(TILES, P, TYPES).transpose(1, 0, 2),
        "ew_t": ew.reshape(TILES, P).T,
        "we_t": we.reshape(TYPES * D, D).T,
        "be": be.reshape(TYPES * D),
        "wih_t": wih.T,
        "whh_t": whh.T,
        "bih": bih.reshape(3, D).T,
        "bhh": bhh.reshape(3, D).T,
        "w1": w1.transpose(1, 0, 2).reshape(D, HEADS * OUT_F),
        "a1": a1.reshape(HEADS, 2, OUT_F).transpose(1, 0, 2),
    }
    nc = bacc.Bacc("TRN2", target_bir_lowering=False, num_devices=1)
    arrays, args = {}, []
    for name in _INS:
        a = np.ascontiguousarray(data[name])
        arrays[f"in_{name}"] = a
        args.append(nc.dram_tensor(f"in_{name}", a.shape, mybir.dt.from_np(a.dtype), kind="ExternalInput").ap())
    args.append(nc.dram_tensor("out_0", (N, D), fp32, kind="ExternalOutput").ap())
    gnn_kernel(nc, *args)
    r = run_bass_kernel_spmd(nc, [arrays], core_ids=[0])
    return r.results[0]["out_0"]
```
